# Optimizing a Trainium2 kernel written in Bass

```python
import numpy as np
import jax
import jax.numpy as jnp

def _softmax(x, axis=-1):
    return jax.nn.softmax(x, axis=axis)

def _gelu(x):
    return jax.nn.gelu(x, approximate=True)

def _silu(x):
    return jax.nn.silu(x)

def _sigmoid(x):
    return jax.nn.sigmoid(x)

def _layernorm(x, axis=-1, eps=1e-05):
    m = jnp.mean(x, axis=axis, keepdims=True)
    v = jnp.var(x, axis=axis, keepdims=True)
    return (x - m) / jnp.sqrt(v + eps)

def _scatter_add(tgt, idx, src, axis=0):
    return tgt.at[idx].add(src)

def _segment_sum(src, seg, n):
    return jax.ops.segment_sum(src, seg, n)
kernel_name = 'mk_early_fusion_d1_tok_img256_r4_e97e09'

def setup_inputs(seed: int=0):
    np.random.seed(seed)
    _w = jnp.asarray

    def _rec_inputs():
        import jax
        import jax.numpy as jnp
        _rk = jax.random.key(seed)
        x = 7.22013e-05 + 1.00017 * jax.random.normal(jax.random.fold_in(_rk, 1), (32, 1, 224, 224), jnp.float32)
        txt = 0.000424648 + 0.582507 * jax.random.normal(jax.random.fold_in(_rk, 2), (32, 32, 64), jnp.float32)
        return (x, txt)
    x, txt = _rec_inputs()

    def _L0_tok_setup():
        import jax, jax.numpy as jnp
        import numpy as np
        P = 8
        C = 1
        D = 64
        key = jax.random.key(seed)
        k1, k2, k3 = jax.random.split(key, 3)
        x = jax.random.normal(k1, (128, C, 64, 64), dtype=jnp.float32)
        patch_dim = P * P * C
        bound = 1.0 / np.sqrt(patch_dim)
        W = jax.random.uniform(k2, (D, patch_dim), dtype=jnp.float32, minval=-bound, maxval=bound)
        b = jax.random.uniform(k3, (D,), dtype=jnp.float32, minval=-bound, maxval=bound)
        return {'x': x, 'W': W, 'b': b}
    _L0_tok_all = _L0_tok_setup()
    _L0_tok_in = {k: v for k, v in _L0_tok_all.items() if k in ('W', 'b')}
    del _L0_tok_all

    def _L0_attn_setup():
        import jax, jax.numpy as jnp
        import numpy as np
        key = jax.random.key(seed)
        ks = jax.random.split(key, 4)
        B, S, D = (4, 1024, 64)
        x = jax.random.normal(ks[0], (B, S, D), dtype=jnp.float32)
        Wq = jax.random.normal(ks[1], (D, D), dtype=jnp.float32) * 0.02
        Wk = jax.random.normal(ks[2], (D, D), dtype=jnp.float32) * 0.02
        Wv = jax.random.normal(ks[3], (D, D), dtype=jnp.float32) * 0.02
        bq = jnp.zeros((D,), dtype=jnp.float32)
        bk = jnp.zeros((D,), dtype=jnp.float32)
        bv = jnp.zeros((D,), dtype=jnp.float32)
        return {'x': x, 'Wq': Wq, 'bq': bq, 'Wk': Wk, 'bk': bk, 'Wv': Wv, 'bv': bv}
    _L0_attn_all = _L0_attn_setup()
    _L0_attn_in = {k: v for k, v in _L0_attn_all.items() if k in ('Wq', 'bq', 'Wk', 'bk', 'Wv', 'bv')}
    del _L0_attn_all

    def _L0_ffn_setup():
        import jax, jax.numpy as jnp
        import numpy as np
        E, D, H, TOP_K = (6, 64, 64, 2)
        ROUTER_H = D // 2
        key = jax.random.key(seed)
        ks = jax.random.split(key, 12)
        s = 1.0 / np.sqrt(D)
        sh = 1.0 / np.sqrt(H)
        sr = 1.0 / np.sqrt(ROUTER_H)
        return {'features': jax.random.normal(ks[0], (8, 1024, D), dtype=jnp.float32), 'router_w1': jax.random.uniform(ks[1], (D, ROUTER_H), jnp.float32, -s, s), 'router_b1': jnp.zeros((ROUTER_H,), jnp.float32), 'router_w2': jax.random.uniform(ks[2], (ROUTER_H, E), jnp.float32, -sr, sr), 'router_b2': jnp.zeros((E,), jnp.float32), 'expert_w1': jax.random.uniform(ks[3], (E, D, H), jnp.float32, -s, s), 'expert_b1': jnp.zeros((E, H), jnp.float32), 'expert_w2': jax.random.uniform(ks[4], (E, H, H), jnp.float32, -sh, sh), 'expert_b2': jnp.zeros((E, H), jnp.float32), 'expert_w3': jax.random.uniform(ks[5], (E, H, D), jnp.float32, -sh, sh), 'expert_b3': jnp.zeros((E, D), jnp.float32)}
    _L0_ffn_all = _L0_ffn_setup()
    _L0_ffn_in = {k: v for k, v in _L0_ffn_all.items() if k in ('router_w1', 'router_b1', 'router_w2', 'router_b2', 'expert_w1', 'expert_b1', 'expert_w2', 'expert_b2', 'expert_w3', 'expert_b3')}
    del _L0_ffn_all
    return {'x': x, 'txt': txt, 'L0_tok_W': _L0_tok_in['W'], 'L0_tok_b': _L0_tok_in['b'], 'L0_attn_Wq': _L0_attn_in['Wq'], 'L0_attn_bq': _L0_attn_in['bq'], 'L0_attn_Wk': _L0_attn_in['Wk'], 'L0_attn_bk': _L0_attn_in['bk'], 'L0_attn_Wv': _L0_attn_in['Wv'], 'L0_attn_bv': _L0_attn_in['bv'], 'L0_ffn_router_w1': _L0_ffn_in['router_w1'], 'L0_ffn_router_b1': _L0_ffn_in['router_b1'], 'L0_ffn_router_w2': _L0_ffn_in['router_w2'], 'L0_ffn_router_b2': _L0_ffn_in['router_b2'], 'L0_ffn_expert_w1': _L0_ffn_in['expert_w1'], 'L0_ffn_expert_b1': _L0_ffn_in['expert_b1'], 'L0_ffn_expert_w2': _L0_ffn_in['expert_w2'], 'L0_ffn_expert_b2': _L0_ffn_in['expert_b2'], 'L0_ffn_expert_w3': _L0_ffn_in['expert_w3'], 'L0_ffn_expert_b3': _L0_ffn_in['expert_b3']}

def reference(x, txt, L0_tok_W, L0_tok_b, L0_attn_Wq, L0_attn_bq, L0_attn_Wk, L0_attn_bk, L0_attn_Wv, L0_attn_bv, L0_ffn_router_w1, L0_ffn_router_b1, L0_ffn_router_w2, L0_ffn_router_b2, L0_ffn_expert_w1, L0_ffn_expert_b1, L0_ffn_expert_w2, L0_ffn_expert_b2, L0_ffn_expert_w3, L0_ffn_expert_b3):
    import jax
    import jax.numpy as jnp

    def _L0_tok_ref(x, W, b):
        import jax, jax.numpy as jnp
        import numpy as np
        P = 8
        C = 1
        D = 64
        B, c, h, w = x.shape
        p = P
        xp = x.reshape(B, c, h // p, p, w // p, p)
        xp = jnp.transpose(xp, (0, 2, 4, 3, 5, 1))
        xp = xp.reshape(B, h // p * (w // p), p * p * c)
        return jnp.einsum('bnk,dk->bnd', xp, W) + b

    def _L0_attn_ref(x, Wq, bq, Wk, bk, Wv, bv):
        import jax, jax.numpy as jnp
        import numpy as np
        Q = jnp.einsum('bsd,de->bse', x, Wq) + bq
        K = jnp.einsum('bsd,de,->bse'.replace(',->', '->'), x, Wk) + bk
        V = jnp.einsum('bsd,de->bse', x, Wv) + bv
        scale = 1.0 / jnp.sqrt(jnp.asarray(Q.shape[-1], dtype=jnp.float32))
        scores = jnp.einsum('bqd,bkd->bqk', Q, K) * scale
        weights = jax.nn.softmax(scores, axis=-1)
        return jnp.einsum('bqk,bkd->bqd', weights, V)

    def _L0_ffn_ref(features, router_w1, router_b1, router_w2, router_b2, expert_w1, expert_b1, expert_w2, expert_b2, expert_w3, expert_b3):
        import jax, jax.numpy as jnp
        import numpy as np
        E, D, H, TOP_K = (6, 64, 64, 2)
        ROUTER_H = D // 2
        rh = jax.nn.relu(features @ router_w1 + router_b1)
        expert_logits = jax.nn.softmax(rh @ router_w2 + router_b2, axis=-1)
        top_w, top_i = jax.lax.top_k(expert_logits, TOP_K)
        routing_weights = jax.nn.softmax(top_w, axis=-1)
        h1 = jax.nn.relu(jnp.einsum('bsd,edh->bseh', features, expert_w1) + expert_b1)
        h2 = jax.nn.relu(jnp.einsum('bseh,ehf->bsef', h1, expert_w2) + expert_b2)
        expert_out = jnp.einsum('bsef,efo->bseo', h2, expert_w3) + expert_b3
        sel = jnp.take_along_axis(expert_out, top_i[:, :, :, None], axis=2)
        combined = jnp.sum(sel * routing_weights[..., None], axis=2)
        return combined
    h = _L0_tok_ref(x, L0_tok_W, L0_tok_b)
    h = jnp.concatenate([h, txt], axis=1)
    h = h + _L0_attn_ref(_layernorm(h, axis=-1), L0_attn_Wq, L0_attn_bq, L0_attn_Wk, L0_attn_bk, L0_attn_Wv, L0_attn_bv)
    h = h + _L0_ffn_ref(_layernorm(h, axis=-1), L0_ffn_router_w1, L0_ffn_router_b1, L0_ffn_router_w2, L0_ffn_router_b2, L0_ffn_expert_w1, L0_ffn_expert_b1, L0_ffn_expert_w2, L0_ffn_expert_b2, L0_ffn_expert_w3, L0_ffn_expert_b3)
    return h

_drawn_inputs = setup_inputs


def setup_inputs(seed=0):
    import zlib

    import numpy as np

    out = dict(_drawn_inputs(seed))
    spreads = {'L0_attn_bq': (0.0, 0.8),
     'L0_attn_bk': (0.0, 0.8),
     'L0_attn_bv': (0.0, 0.1),
     'L0_ffn_router_b1': (0.0, 0.1),
     'L0_ffn_router_b2': (0.0, 0.1),
     'L0_ffn_expert_b1': (0.0, 0.407),
     'L0_ffn_expert_b2': (0.0, 0.1),
     'L0_ffn_expert_b3': (0.0, 0.1)}
    factors = {'L0_attn_Wq': 8.0, 'L0_attn_Wk': 8.0}
    for name, (base, spread) in spreads.items():
        noise = np.random.default_rng([zlib.crc32(name.encode()), seed]).standard_normal(out[name].shape)
        drawn = base * np.exp(spread * noise) if base else spread * noise
        out[name] = jnp.asarray(drawn.astype(out[name].dtype))
    for name, factor in factors.items():
        out[name] = (out[name] * factor).astype(out[name].dtype)
    return out
```

```python
from contextlib import ExitStack

import concourse.bass as bass
from concourse import mybir

F32 = mybir.dt.float32
F32R = mybir.dt.float32r
ALU = mybir.AluOpType
ACT = mybir.ActivationFunctionType
AX = mybir.AxisListType

P = 128
BATCH = 32
D = 64
IMG = 224
PATCH = 8
SIDE = IMG // PATCH
WP2 = SIDE // 4
HROW = IMG // 2
TXT = 32
NIMG = SIDE * SIDE // 2
TOK = SIDE * SIDE + TXT
HALF = TOK // 2
ROWS = 102
TT = HALF // ROWS
G = 2 * TT
NT = -(-TOK // P)
E_ = 6
RH = 32
PAIRS = E_ // 2
CHUNKS = 2 * PAIRS
EPS = 1e-5
SCALE = D ** -0.5
BIG = 3.0e38
RING = 3
LAG = dict(X=0, E=1, A=2, B=3, P=4, F=5)
DEPTH = max(LAG.values())
WORK = 5


def width(t):
    return min(P, TOK - P * t)


def score_tiles(j):
    return {0: (0, 1), NT - 1: ()}.get(j, (j + 1,))


def bank_users(j):
    out = []
    if j < CHUNKS:
        out += [("F", "spread", j), ("F", "hidden1", j)]
    out += [("B", "scores_t", j, 0), ("B", "scores_t", j, 1)]
    if j < CHUNKS:
        out += [("F", "hidden2", j)]
    out += [("A", "scores", t, h) for t in score_tiles(j) for h in (0, 1)]
    out += {
        0: [("E", "embed"), ("P", "attn", 0), ("P", "attn", 1)],
        1: [("E", "tokens")],
        2: [("X", "patches")],
        3: [("P", "norm2", 0), ("P", "norm2", 1)],
        4: [("P", "router", 0), ("P", "router", 1), ("E", "norm1", 0), ("E", "norm1", 1)],
        5: [("P", "logits"), ("E", "query", 0), ("E", "query", 1)],
        6: [("A", "shifted", 0), ("A", "shifted", 1), ("E", "values"), ("F", "back"),
            ("P", "weights", 0), ("P", "weights", 1)],
    }[j]
    return out


class Use:

    def __init__(self, bank, filled, drained, step):
        self.bank, self.filled_at, self.drained_at, self.step = bank, filled, drained, step

    def filled(self):
        return self.filled_at + self.step.turn * self.step.filled_per_turn

    def drained(self):
        return self.drained_at + self.step.turn * self.step.drained_per_turn[self.bank]

    def read(self):
        return self.drained() + 1


class Step:

    def __init__(self, at, turn=0):
        self.at, self.turn = at, turn

    def runs(self, stage):
        return 0 <= self.at - LAG[stage] < BATCH

    def ring(self, stage):
        return (self.at - LAG[stage]) % RING

    def image(self, stage):
        return self.at - LAG[stage] + RING * self.turn

    def has(self, stage, back):
        return self.at - LAG[stage] - back >= 0

    def count(self, stage, each, part=None, back=0):
        b = self.at - LAG[stage] - back
        return b * each + (each if part is None else part) + self.turn * (RING * each)

    def ring_dma(self, stage, back=0):
        return 16 * ((self.at - LAG[stage] - back) // RING + 1) + self.turn * 16


FIRST_LOOPED = DEPTH + 1
TURNS = (BATCH - FIRST_LOOPED) // RING
AFTER_LOOP = FIRST_LOOPED + TURNS * RING
LAST = BATCH + DEPTH


def plan():
    uses, filled, drained = {}, 0, [0] * WORK
    in_step = [name for j in range(NT) for name in bank_users(j)]

    def walk(steps):
        nonlocal filled
        for s in steps:
            at = (s - FIRST_LOOPED) % RING * len(in_step)
            for n, (stage, *name) in enumerate(in_step):
                if Step(s).runs(stage):
                    bank = (at + n) % WORK
                    uses[s, tuple(name)] = (bank, filled + 1, drained[bank])
                    filled += 1
                    drained[bank] += 1

    walk(range(FIRST_LOOPED))
    before, were = filled, list(drained)
    walk(range(FIRST_LOOPED, FIRST_LOOPED + RING))
    per_turn = filled - before
    drained_per_turn = [a - b for a, b in zip(drained, were)]
    filled += (TURNS - 1) * per_turn
    for k in range(WORK):
        drained[k] += (TURNS - 1) * drained_per_turn[k]
    walk(range(AFTER_LOOP, LAST))
    return uses, per_turn, drained_per_turn


USES, FILLED_PER_TURN, DRAINED_PER_TURN = plan()
Step.filled_per_turn = FILLED_PER_TURN
Step.drained_per_turn = DRAINED_PER_TURN


def use(step, *name):
    return Use(*USES[step.at, name], step)


def last_use(step, *name):
    if step.at != AFTER_LOOP and step.at != FIRST_LOOPED:
        return Use(*USES[step.at - 1, name], step)
    turns = 1 if step.at == FIRST_LOOPED else 1 - TURNS
    at = FIRST_LOOPED + RING - 1
    bank, filled, drained = USES[at, name]
    return Use(bank, filled - turns * FILLED_PER_TURN, drained - turns * DRAINED_PER_TURN[bank], step)


for _name in (("query", 1), ("shifted", 1), ("weights", 1), ("values",)):
    _u = last_use(Step(FIRST_LOOPED), *_name)
    assert (_u.bank, _u.filled_at, _u.drained_at) == USES[FIRST_LOOPED - 1, _name]


def run_steps(eng, body):
    for s in range(FIRST_LOOPED):
        body(Step(s))
    with eng.Fori(0, TURNS) as turn:
        for u in range(RING):
            body(Step(FIRST_LOOPED + u, turn))
    for s in range(AFTER_LOOP, LAST):
        body(Step(s))


def encoder_kernel(nc, x, txt, tok_W, tok_b, Wq, bq, Wk, bk, Wv, bv, r_w1, r_b1, r_w2, r_b2,
                   e_w1, e_b1, e_w2, e_b2, e_w3, e_b3, out):
    ctx = ExitStack()
    with ctx:
        def sb(name, shape, dt=F32):
            return ctx.enter_context(nc.sbuf_tensor(name, shape, dt))

        def sem(name):
            return ctx.enter_context(nc.semaphore(name))

        work = [ctx.enter_context(nc.psum_tensor(f"work{k}", [P, 512], F32)) for k in range(WORK)]
        ps_attn = ctx.enter_context(nc.psum_tensor("ps_attn", [P, 2, 512], F32))
        ps_moe = ctx.enter_context(nc.psum_tensor("ps_moe", [P, 512], F32))

        ident = sb("ident", [P, P])
        ones_r = sb("ones_r", [P, P], F32R)
        center = sb("center", [D + 1, 2 * D])
        prio = sb("prio", [P, E_])
        minus_half = sb("minus_half", [P, G])
        one_of_d = sb("one_of_d", [P, G])
        eps = sb("eps", [P, G])
        raw_tok = sb("raw_tok", [D, 2 * D])
        tok_bias = sb("tok_bias", [P, 1])
        embed_w = sb("embed_w", [P, P])
        NF = 2 * D + 2 * RH + E_ * D
        QC, VC, RC, EC = 0, D, 2 * D, 2 * D + 2 * RH
        raw_first = sb("raw_first", [D + 1, NF])
        raw_k = sb("raw_k", [D + 1, D])
        query_t = sb("query_t", [D, 2 * D])
        key_t = sb("key_t", [D, 2 * D])
        score_w = [sb("score_w_hi", [P, P], F32R), sb("score_w_lo", [P, P], F32R)]
        first_w = [sb("first_w_hi", [P, NF], F32R), sb("first_w_lo", [P, NF], F32R)]
        w2 = sb("w2", [P, PAIRS, P])
        b2 = sb("b2", [P, PAIRS])
        w3 = sb("w3", [P, PAIRS, D])
        raw_r2 = sb("raw_r2", [2 * RH, E_])
        router2 = sb("router2", [2 * RH, 2 * E_], F32R)
        router_bias = sb("router_bias", [ROWS, E_])
        raw_b3 = sb("raw_b3", [4 * E_, D])
        b3_hi = sb("b3_hi", [4 * E_, D], F32R)
        b3_lo = sb("b3_lo", [4 * E_, D])
        b3_low_rows = sb("b3_low_rows", [4 * E_, D])
        is_hi_row = sb("is_hi_row", [4 * E_, D])
        is_lo_row = sb("is_lo_row", [4 * E_, D])
        b3 = sb("b3", [4 * E_, D], F32R)
        raw_pick = sb("raw_pick", [4 * E_, PAIRS, 2, D])
        pick = sb("pick", [4 * E_, PAIRS * P], F32R)

        pixels = sb("pixels", [2 * SIDE, RING, PATCH * HROW])
        by_patch = sb("by_patch", [2 * SIDE, PATCH * HROW])
        text = sb("text", [TXT // 2, RING, 2 * D])
        patches = sb("patches", [P, NIMG])
        embed_t = sb("embed_t", [P, HALF])
        h1 = sb("h1", [ROWS, RING, G * D])
        stat = {k: [sb(f"{n}{k}", [ROWS, G]) for n in ("total", "mean", "squares", "var", "rstd")]
                for k in (1, 2)}
        xc = {k: sb(f"xc{k}", [ROWS, G * D]) for k in (1, 2)}
        sq = {k: sb(f"sq{k}", [ROWS, G * D]) for k in (1, 2)}
        xn = {k: sb(f"xn{k}", [ROWS, G, 2 * D]) for k in (1, 2)}
        pair1 = sb("pair1", [P, RING, TOK], F32R)
        pair2 = sb("pair2", [P, RING, TOK], F32R)
        query_hi = sb("query_hi", [P, RING, TOK], F32R)
        values = sb("values", [P, RING, NT, D + 1])
        row_max = sb("row_max", [P, NT, 2])
        minus_max = sb("minus_max", [P, NT])
        max_diag = sb("max_diag", [P, TOK], F32R)
        shifted = [sb("shifted_hi", [P, RING, TOK], F32R), sb("shifted_lo", [P, RING, TOK], F32R)]
        probs = sb("probs", [P, 3, TOK])
        attn_t = sb("attn_t", [D + 1, TOK])
        inv_sum = sb("inv_sum", [ROWS, G])
        attn = sb("attn", [ROWS, G * D])
        h2 = sb("h2", [ROWS, RING, G * D])
        routed = sb("routed", [2 * RH, TOK], F32R)
        lg = sb("lg", [ROWS, G, E_])
        lg_hi = sb("lg_hi", [ROWS, G, E_])
        lg_rest = sb("lg_rest", [ROWS, G, E_])
        best = sb("best", [ROWS, 2, G])
        tie = sb("tie", [ROWS, G, E_])
        first_tie = sb("first_tie", [ROWS, G])
        chosen = sb("chosen", [ROWS, 2, G, E_])
        expo = sb("expo", [ROWS, G, E_ + 1])
        expo_sum = sb("expo_sum", [ROWS, G])
        expo_inv = sb("expo_inv", [ROWS, G])
        gap = sb("gap", [ROWS, G])
        gap_exp = sb("gap_exp", [ROWS, G])
        share = sb("share", [ROWS, 2, G])
        wsum = sb("wsum", [ROWS, 2, G, E_])
        wts = sb("wts", [ROWS, G, E_])
        wts_hi = sb("wts_hi", [ROWS, G, E_], F32R)
        wts_pair = sb("wts_pair", [ROWS, G, 4 * E_])
        weights_t = sb("weights_t", [4 * E_, RING, TOK], F32R)
        act1 = sb("act1", [P, 2, HALF])
        act2 = sb("act2", [P, 2, HALF])
        scaled = sb("scaled", [P, 2, HALF])
        moe_t = sb("moe_t", [D, TOK])
        result = sb("result", [ROWS, RING, G * D])

        weights_loaded = sem("weights_loaded")
        consts_made = sem("consts_made")
        prep_filled = sem("prep_filled")
        prep_copied = sem("prep_copied")
        pixels_loaded = [sem(f"pixels_loaded{k}") for k in range(RING)]
        text_loaded = [sem(f"text_loaded{k}") for k in range(RING)]
        stored = [sem(f"stored{k}") for k in range(RING)]
        filled = sem("filled")
        drained = [sem(f"drained{k}") for k in range(WORK)]
        by_patch_ready = sem("by_patch_ready")
        patches_ready = sem("patches_ready")
        total_ready = {k: sem(f"total_ready{k}") for k in (1, 2)}
        norm_step = {k: sem(f"norm_step{k}") for k in (1, 2)}
        sq_ready = {k: sem(f"sq_ready{k}") for k in (1, 2)}
        squares_ready = {k: sem(f"squares_ready{k}") for k in (1, 2)}
        hi1_ready = sem("hi1_ready")
        hi2_ready = sem("hi2_ready")
        max_ready = sem("max_ready")
        diag_ready = sem("diag_ready")
        shifted_hi = sem("shifted_hi")
        attended = sem("attended")
        attn_copied = sem("attn_copied")
        sums_inverted = sem("sums_inverted")
        h2_ready = sem("h2_ready")
        routed_hi = sem("routed_hi")
        route_step = sem("route_step")
        expo_ready = sem("expo_ready")
        gap_ready = sem("gap_ready")
        chunk_done = sem("chunk_done")
        moe_copied = sem("moe_copied")
        EXPO_AT, GAP_AT, ROUTE = 14, 17, 25
        N_LOADS = 33
        N_CONSTS = 17 + E_
        N_PREP = 20

        block = ctx.enter_context(nc.Block())

        def groups(ap):
            return ap.rearrange("p (g d) -> p g d", d=D)

        def wide(stat_ap, n=D):
            return stat_ap.unsqueeze(2).broadcast_to([ROWS, G, n])

        def wait_read(eng, u):
            eng.wait_ge(drained[u.bank], u.read())

        @block.sync
        def _(sp):
            def load(dst, src):
                sp.dma_start(dst, src).then_inc(weights_loaded, 16)

            for k in range(2):
                load(raw_tok[:, k * D:(k + 1) * D], tok_W)
                load(tok_bias[k * D:(k + 1) * D, :], tok_b.rearrange("(d o) -> d o", o=1))
            for c, (w, b) in ((QC, (Wq, bq)), (VC, (Wv, bv)), (RC, (r_w1, r_b1)), (RC + RH, (r_w1, r_b1))):
                n = w.shape[1]
                load(raw_first[0:D, c:c + n], w)
                load(raw_first[D:D + 1, c:c + n], b.rearrange("(o d) -> o d", o=1))
            load(raw_first[0:D, EC:NF].rearrange("p (e h) -> p e h", e=E_), e_w1.rearrange("e d h -> d e h"))
            load(raw_first[D:D + 1, EC:NF], e_b1.rearrange("(o e) h -> o (e h)", o=1))
            load(raw_k[0:D, :], Wk)
            load(raw_k[D:D + 1, :], bk.rearrange("(o d) -> o d", o=1))
            sp.wait_ge(consts_made, 2)
            for k in range(2):
                load(w2[k * D:(k + 1) * D, :, k * D:(k + 1) * D],
                     e_w2.rearrange("(q k) h f -> k h q f", k=2)[k])
                for q in range(PAIRS):
                    load(b2[k * D:(k + 1) * D, q:q + 1], e_b2[2 * q + k].rearrange("(f o) -> f o", o=1))
                load(w3[k * D:(k + 1) * D, :, :], e_w3.rearrange("(q k) f o -> k f q o", k=2)[k])
                load(raw_r2[k * RH:(k + 1) * RH, :], r_w2)
            load(router_bias[:, :], r_b2.rearrange("(o e) -> o e", o=1).broadcast_to([ROWS, E_]))
            for k in range(4):
                load(raw_b3[k * E_:(k + 1) * E_, :], e_b3)

            def load_image(S):
                if S.has("X", RING):
                    sp.wait_ge(by_patch_ready, S.count("X", 1, back=RING))
                    sp.wait_ge(patches_ready, S.count("X", 1, back=RING))
                b = S.image("X")
                k = S.ring("X")
                rows = x[b, 0].rearrange("(r p) w -> r p w", p=PATCH)
                for h in range(2):
                    sp.dma_start(pixels[h * SIDE:(h + 1) * SIDE, k, :].rearrange("r (p w) -> r p w", p=PATCH),
                                 rows[:, :, h * HROW:(h + 1) * HROW]).then_inc(pixels_loaded[k], 16)
                sp.dma_start(text[:, k, :], txt[b].rearrange("(r p) d -> r (p d)", p=2)
                             ).then_inc(text_loaded[k], 16)

            def body(S):
                if S.runs("X"):
                    load_image(S)
                if S.runs("F"):
                    b = S.image("F")
                    k = S.ring("F")
                    wait_read(sp, use(S, "back"))
                    sp.dma_start(out[b].rearrange("(t r p) d -> r t (p d)", t=TT, r=ROWS),
                                 result[:, k, :].rearrange("r (t q) -> r t q", t=TT)
                                 ).then_inc(stored[k], 16)

            run_steps(sp, body)
            for k in range(RING):
                sp.wait_ge(stored[k], 16 * len(range(k, BATCH, RING)))

        @block.gpsimd
        def _(pool):
            pool.memset(center[D:D + 1, :], 1.0).then_inc(consts_made, 1)
            pool.wait_ge(consts_made, 1)
            pool.memset(w2[:, :, :], 0.0).then_inc(consts_made, 1)
            pool.memset(embed_w[:, :], 0.0).then_inc(consts_made, 1)
            pool.memset(ident[:, :], 0.0).then_inc(consts_made, 1)
            pool.memset(center[0:D, :], -1.0 / D).then_inc(consts_made, 1)
            pool.memset(raw_pick[:, :, :, :], 0.0).then_inc(consts_made, 1)
            pool.memset(is_hi_row[:, :], 1.0).then_inc(consts_made, 1)
            pool.memset(minus_half[:, :], -0.5).then_inc(consts_made, 1)
            pool.memset(one_of_d[:, :], 1.0 / D).then_inc(consts_made, 1)
            pool.memset(eps[:, :], EPS).then_inc(consts_made, 1)
            for e in range(E_):
                pool.memset(prio[:, e:e + 1], float(E_ - e)).then_inc(consts_made, 1)
            pool.memset(values[:, :, :, :], 1.0).then_inc(consts_made, 1)
            pool.memset(max_diag[:, :].bitcast(F32), 0.0).then_inc(consts_made, 1)
            made = 12 + E_
            pool.wait_ge(consts_made, made)
            pool.affine_select(out=ident[:, :], in_=ident[:, :], compare_op=ALU.not_equal, fill=1.0,
                               base=0, pattern=[[-1, P]], channel_multiplier=1).then_inc(consts_made, 1)
            pool.affine_select(out=center[0:D, :].rearrange("p (k d) -> p k d", k=2),
                               in_=center[0:D, :].rearrange("p (k d) -> p k d", k=2),
                               compare_op=ALU.not_equal, fill=1.0 - 1.0 / D, base=0,
                               pattern=[[0, 2], [-1, D]], channel_multiplier=1).then_inc(consts_made, 1)
            pool.affine_select(out=is_hi_row[:, :], in_=is_hi_row[:, :], compare_op=ALU.is_ge, fill=0.0,
                               base=2 * E_ - 1, pattern=[[0, D]], channel_multiplier=-1
                               ).then_inc(consts_made, 1)
            for k in range(2):
                pool.affine_select(out=raw_pick[:, :, :, :], in_=raw_pick[:, :, :, :],
                                   compare_op=ALU.not_equal, fill=1.0, base=-E_ * k,
                                   pattern=[[-2, PAIRS], [-1, 2], [0, D]], channel_multiplier=1
                                   ).then_inc(consts_made, 1)
                pool.wait_ge(consts_made, made + 4 + k)

            def norm(S, stage, k, x_ap):
                step = norm_step[k]
                total, mean, _, _, _ = stat[k]
                pool.wait_ge(total_ready[k], S.count(stage, 1))
                if S.has(stage, 1):
                    pool.wait_ge(squares_ready[k], S.count(stage, 1, back=1))
                pool.tensor_tensor(mean[:, :], total[:, :], one_of_d[0:ROWS, :], ALU.mult).then_inc(step, 1)
                pool.wait_ge(step, S.count(stage, 6, 1))
                pool.tensor_tensor(groups(xc[k][:, :]), groups(x_ap), wide(mean[:, :]), ALU.subtract
                                   ).then_inc(step, 1)

            def norm_end(S, stage, k):
                step = norm_step[k]
                _, _, squares, var, rstd = stat[k]
                pool.wait_ge(squares_ready[k], S.count(stage, 1))
                pool.tensor_tensor(var[:, :], squares[:, :], one_of_d[0:ROWS, :], ALU.mult).then_inc(step, 1)
                pool.wait_ge(step, S.count(stage, 6, 3))
                pool.tensor_tensor(var[:, :], var[:, :], eps[0:ROWS, :], ALU.add).then_inc(step, 1)
                pool.wait_ge(step, S.count(stage, 6, 4))
                pool.tensor_tensor(rstd[:, :], var[:, :], minus_half[0:ROWS, :], ALU.pow).then_inc(step, 1)
                pool.wait_ge(step, S.count(stage, 6, 5))
                if S.has(stage, 1):
                    pool.wait_ge({1: hi1_ready, 2: hi2_ready}[k], S.count(stage, 2, back=1))
                both = [ROWS, G, 2, D]
                pool.tensor_tensor(xn[k][:, :, :].rearrange("p g (k d) -> p g k d", k=2),
                                   groups(xc[k][:, :]).unsqueeze(2).broadcast_to(both),
                                   rstd[:, :].unsqueeze(2).unsqueeze(3).broadcast_to(both), ALU.mult
                                   ).then_inc(step, 1)

            def body(S):
                for j in range(NT):
                    if S.runs("A"):
                        for t in score_tiles(j):
                            n = width(t)
                            pool.wait_ge(max_ready, S.count("A", NT, t + 1))
                            if t == 0 and S.has("A", 1):
                                pool.wait_ge(shifted_hi, S.count("A", 2, back=1))
                            pool.tensor_tensor(max_diag[0:n, t * P:t * P + n], ident[0:n, 0:n],
                                               minus_max[0:n, t:t + 1].broadcast_to([n, n]), ALU.mult
                                               ).then_inc(diag_ready, 1)
                    if j == 0 and S.runs("P"):
                        for i in range(2):
                            wait_read(pool, use(S, "attn", i))
                        pool.tensor_tensor(h2[:, S.ring("P"), :], attn[:, :], h1[:, S.ring("P"), :],
                                           ALU.add).then_inc(h2_ready, 1)
                    if j == 1 and S.runs("P"):
                        norm(S, "P", 2, h2[:, S.ring("P"), :])
                    if j == 2:
                        if S.runs("P"):
                            norm_end(S, "P", 2)
                        if S.runs("E"):
                            norm(S, "E", 1, h1[:, S.ring("E"), :])
                    if j == 3 and S.runs("E"):
                        norm_end(S, "E", 1)

            run_steps(pool, body)

        @block.tensor
        def _(pe):
            pe.wait_ge(weights_loaded, 16 * N_LOADS)
            pe.wait_ge(consts_made, N_CONSTS)
            pe.transpose(ps_moe[:, 0:D], raw_tok[:, :], ident[0:D, 0:D])
            pe.matmul(ps_moe[0:D, P:2 * P], raw_first[:, QC:QC + D], center[:, :], start=True, stop=True)
            pe.matmul(ps_moe[0:D, 2 * P:3 * P], raw_k[:, :], center[:, :], start=True, stop=True)
            pe.matmul(ps_attn[:, 0, 0:EC], center[:, :], raw_first[:, 0:EC], start=True, stop=True)
            pe.matmul(ps_attn[:, 1, 0:NF - EC], center[:, :], raw_first[:, EC:NF], start=True, stop=True
                      ).then_inc(prep_filled, 1)
            pe.wait_ge(prep_copied, 4)
            pe.matmul(work[0][:, 0:P], query_t[:, :], key_t[:, :], start=True, stop=True
                      ).then_inc(prep_filled, 1)
            pe.wait_ge(prep_copied, N_PREP)

            def take(S, *name, after=()):
                u = use(S, *name)
                least = {u.bank: u.drained()} if u.drained_at > 0 else {}
                for v in after:
                    if v.bank != u.bank or v.drained_at + 1 > u.drained_at:
                        least[v.bank] = v.read()
                for bank, count in least.items():
                    pe.wait_ge(drained[bank], count)
                return work[u.bank]

            def two_passes(dst, w, c, n, rhs):
                pe.matmul(dst, w[0][:, c:c + n], rhs, start=True, stop=False)
                return pe.matmul(dst, w[1][:, c:c + n], rhs, start=False, stop=True)

            def attend(S, t):
                n = width(t)
                for h in range(2):
                    wait_read(pe, use(S, "scores_t", t, h))
                    if t == 0 and S.has("B", 1):
                        pe.wait_ge(attn_copied, S.count("B", 2, h + 1, back=1))
                    pe.matmul(ps_attn[0:D + 1, h, 0:HALF], values[0:n, S.ring("B"), t, :],
                              probs[0:n, t % 3, h * HALF:(h + 1) * HALF],
                              start=(t == 0), stop=(t == NT - 1)).then_inc(attended, 1)

            def experts_out(S, c):
                h, q = divmod(c, PAIRS)
                wait_read(pe, use(S, "spread", c))
                if q == 0 and (h == 1 or S.has("F", 1)):
                    pe.wait_ge(moe_copied, S.count("F", 2, h, back=0))
                pe.matmul(ps_moe[0:D, 0:HALF], w3[:, q, :], scaled[:, c % 2, :], start=(q == 0), stop=False)
                if q == PAIRS - 1:
                    pe.matmul(ps_moe[0:D, 0:HALF], b3[:, :],
                              weights_t[:, S.ring("F"), h * HALF:(h + 1) * HALF],
                              start=False, stop=True).then_inc(chunk_done, 1)

            def body(S):
                for j in range(NT):
                    if j < CHUNKS and S.runs("F"):
                        h, q = divmod(j, PAIRS)
                        cols = slice(h * HALF, (h + 1) * HALF)
                        k = S.ring("F")
                        bank = take(S, "spread", j, after=[last_use(S, "weights", h)])
                        pe.matmul(bank[:, 0:HALF], pick[:, q * P:(q + 1) * P], weights_t[:, k, cols],
                                  start=True, stop=True).then_inc(filled, 1)
                        bank = take(S, "hidden1", j)
                        two_passes(bank[:, 0:HALF], first_w, EC + q * P, P, pair2[:, k, cols]
                                   ).then_inc(filled, 1)
                    if S.runs("B"):
                        n, k = width(j), S.ring("B")
                        for h in range(2):
                            bank = take(S, "scores_t", j, h,
                                        after=[last_use(S, "shifted", h)] if j == 0 else [])
                            for part in range(2):
                                mm = pe.matmul(bank[0:n, 0:HALF], pair1[:, k, j * P:j * P + n],
                                               shifted[part][:, k, h * HALF:(h + 1) * HALF],
                                               start=(part == 0), stop=(part == 1))
                            mm.then_inc(filled, 1)
                    if j < CHUNKS and S.runs("F"):
                        h, q = divmod(j, PAIRS)
                        bank = take(S, "hidden2", j, after=[use(S, "hidden1", j)])
                        pe.matmul(bank[:, 0:HALF], w2[:, q, :], act1[:, j % 2, :], start=True, stop=True
                                  ).then_inc(filled, 1)
                    if j >= 1 and S.runs("B"):
                        attend(S, j - 1)
                    if j < CHUNKS and S.runs("F"):
                        experts_out(S, j)
                    if S.runs("A"):
                        k = S.ring("A")
                        for t in score_tiles(j):
                            n = width(t)
                            for h in range(2):
                                bank = take(S, "scores", t, h, after=[
                                    last_use(S, "query", 0), last_use(S, "query", 1), last_use(S, "values")
                                ] if (t, h) == (0, 0) else [])
                                pe.matmul(bank[0:n, 0:HALF], query_hi[:, k, t * P:t * P + n],
                                          pair1[:, k, h * HALF:(h + 1) * HALF],
                                          start=True, stop=True).then_inc(filled, 1)
                    if j == 0 and S.runs("E"):
                        pe.wait_ge(patches_ready, S.count("E", 1))
                        bank = take(S, "embed")
                        pe.matmul(bank[:, 0:NIMG], embed_w[:, :], patches[:, :], start=True, stop=True
                                  ).then_inc(filled, 1)
                    if j == 0 and S.runs("P"):
                        pe.wait_ge(attn_copied, S.count("P", 2))
                        for i in range(2):
                            bank = take(S, "attn", i)
                            for g in range(G // 2):
                                c = (i * (G // 2) + g) * ROWS
                                mm = pe.transpose(bank[0:ROWS, g * (D + 1):(g + 1) * (D + 1)],
                                                  attn_t[:, c:c + ROWS], ident[0:D + 1, 0:D + 1])
                            mm.then_inc(filled, 1)
                    if j == 1 and S.runs("E"):
                        bank = take(S, "tokens", after=[use(S, "embed")])
                        for t in range(TT):
                            mm = pe.transpose(bank[0:ROWS, t * P:(t + 1) * P],
                                              embed_t[:, t * ROWS:(t + 1) * ROWS], ident[:, :])
                        mm.then_inc(filled, 1)
                    if j == 2 and S.runs("X"):
                        k = S.ring("X")
                        pe.wait_ge(by_patch_ready, S.count("X", 1))
                        pe.wait_ge(text_loaded[k], S.ring_dma("X"))
                        bank = take(S, "patches")
                        n = 2 * SIDE
                        pe.matmul(bank[:, 0:n], by_patch[:, 0:P], ident[0:n, 0:n], start=True, stop=True)
                        for w in range(1, WP2):
                            pe.transpose(bank[:, w * n:(w + 1) * n], by_patch[:, w * P:(w + 1) * P],
                                         ident[0:n, 0:n])
                        pe.transpose(bank[:, NIMG:HALF], text[:, k, :], ident[0:TXT // 2, 0:TXT // 2]
                                     ).then_inc(filled, 1)
                    if j == 3 and S.runs("P"):
                        pe.wait_ge(norm_step[2], S.count("P", 6))
                        turn_tokens(S, "norm2", xn[2])
                    if j == 4 and S.runs("P"):
                        k = S.ring("P")
                        for h in range(2):
                            bank = take(S, "router", h, after=[use(S, "norm2", h)])
                            two_passes(bank[0:2 * RH, 0:HALF], first_w, RC, 2 * RH,
                                       pair2[:, k, h * HALF:(h + 1) * HALF]).then_inc(filled, 1)
                    if j == 4 and S.runs("E"):
                        pe.wait_ge(norm_step[1], S.count("E", 6))
                        turn_tokens(S, "norm1", xn[1])
                    if j == 5 and S.runs("P"):
                        bank = take(S, "logits", after=[use(S, "router", 0), use(S, "router", 1)])
                        for g in range(G):
                            mm = pe.matmul(bank[0:ROWS, g * 2 * E_:(g + 1) * 2 * E_],
                                           routed[:, g * ROWS:(g + 1) * ROWS], router2[:, :],
                                           start=True, stop=True)
                        mm.then_inc(filled, 1)
                    if j == 5 and S.runs("E"):
                        k = S.ring("E")
                        for h in range(2):
                            bank = take(S, "query", h, after=[use(S, "norm1", h)])
                            two_passes(bank[:, 0:HALF], score_w, 0, P, pair1[:, k, h * HALF:(h + 1) * HALF]
                                       ).then_inc(filled, 1)
                    if j == 6:
                        if S.runs("A"):
                            k = S.ring("A")
                            pe.wait_ge(diag_ready, S.count("A", NT))
                            for h in range(2):
                                cols = slice(h * HALF, (h + 1) * HALF)
                                bank = take(S, "shifted", h)
                                for part in range(2):
                                    pe.matmul(bank[:, 0:HALF], score_w[part][:, :], pair1[:, k, cols],
                                              start=(part == 0), stop=False)
                                pe.matmul(bank[:, 0:HALF], ones_r[:, :], max_diag[:, cols],
                                          start=False, stop=True).then_inc(filled, 1)
                        if S.runs("E"):
                            k = S.ring("E")
                            bank = take(S, "values")
                            for t in range(NT):
                                n = width(t)
                                for part in range(2):
                                    mm = pe.matmul(bank[0:n, t * D:(t + 1) * D],
                                                   pair1[:, k, t * P:t * P + n],
                                                   first_w[part][:, VC:VC + D],
                                                   start=(part == 0), stop=(part == 1))
                            mm.then_inc(filled, 1)
                        if S.runs("F"):
                            pe.wait_ge(moe_copied, S.count("F", 2))
                            bank = take(S, "back")
                            pe.matmul(bank[0:ROWS, 0:D], moe_t[:, 0:ROWS], ident[0:D, 0:D],
                                      start=True, stop=True)
                            for g in range(1, G):
                                mm = pe.transpose(bank[0:ROWS, g * D:(g + 1) * D],
                                                  moe_t[:, g * ROWS:(g + 1) * ROWS], ident[0:D, 0:D])
                            mm.then_inc(filled, 1)
                        if S.runs("B"):
                            attend(S, NT - 1)
                        if S.runs("P"):
                            pe.wait_ge(route_step, S.count("P", ROUTE))
                            for i in range(2):
                                bank = take(S, "weights", i)
                                for g in range(G // 2):
                                    mm = pe.transpose(bank[0:4 * E_, g * ROWS:(g + 1) * ROWS],
                                                      wts_pair[:, i * (G // 2) + g, :],
                                                      ident[0:ROWS, 0:ROWS])
                                mm.then_inc(filled, 1)

            def turn_tokens(S, name, src):
                for i in range(2):
                    bank = take(S, name, i)
                    for g in range(G // 2):
                        mm = pe.transpose(bank[:, g * ROWS:(g + 1) * ROWS], src[:, i * (G // 2) + g, :],
                                          ident[0:ROWS, 0:ROWS])
                    mm.then_inc(filled, 1)

            run_steps(pe, body)

        @block.scalar
        def _(act):
            act.wait_ge(weights_loaded, 16 * N_LOADS)

            def body(S):
                for j in range(NT):
                    if j < CHUNKS and S.runs("F"):
                        u = use(S, "hidden1", j)
                        act.wait_ge(filled, u.filled())
                        act.activation(act1[:, j % 2, :], work[u.bank][:, 0:HALF], ACT.Relu
                                       ).then_inc(drained[u.bank], 1)
                    if S.runs("B"):
                        n = width(j)
                        for h in range(2):
                            u = use(S, "scores_t", j, h)
                            act.wait_ge(filled, u.filled())
                            act.activation(probs[0:n, j % 3, h * HALF:(h + 1) * HALF],
                                           work[u.bank][0:n, 0:HALF], ACT.Exp, scale=SCALE
                                           ).then_inc(drained[u.bank], 1)
                    if S.runs("F"):
                        if j in (PAIRS, NT - 1):
                            h = 0 if j == PAIRS else 1
                            act.wait_ge(chunk_done, S.count("F", 2, h + 1))
                            act.activation(moe_t[:, h * HALF:(h + 1) * HALF], ps_moe[0:D, 0:HALF], ACT.Copy
                                           ).then_inc(moe_copied, 1)
                        if j < CHUNKS:
                            u = use(S, "hidden2", j)
                            act.wait_ge(filled, u.filled())
                            act.activation(act2[:, j % 2, :], work[u.bank][:, 0:HALF], ACT.Relu,
                                           bias=b2[:, j % PAIRS:j % PAIRS + 1]
                                           ).then_inc(drained[u.bank], 1)
                    if j == 0 and S.runs("E"):
                        u = use(S, "embed")
                        act.wait_ge(filled, u.filled())
                        act.activation(embed_t[:, 0:NIMG], work[u.bank][:, 0:NIMG], ACT.Identity,
                                       bias=tok_bias[:, :]).then_inc(drained[u.bank], 1)
                    if j == 1 and S.runs("E"):
                        u = use(S, "tokens")
                        act.wait_ge(filled, u.filled())
                        if S.has("E", RING):
                            act.wait_ge(h2_ready, S.count("E", 1, back=RING))
                        act.activation(h1[:, S.ring("E"), :], work[u.bank][0:ROWS, :], ACT.Copy
                                       ).then_inc(drained[u.bank], 1)
                    if j == 2:
                        if S.runs("P"):
                            square(S, "P", 2)
                        if S.runs("X"):
                            u = use(S, "patches")
                            act.wait_ge(filled, u.filled())
                            act.activation(patches[:, :].rearrange("p (r h w) -> p w h r", h=2, w=WP2),
                                           work[u.bank][:, 0:NIMG].rearrange("p (w h r) -> p w h r", h=2, w=WP2),
                                           ACT.Copy).then_inc(patches_ready, 1)
                            act.activation(embed_t[:, NIMG:HALF], work[u.bank][:, NIMG:HALF], ACT.Copy
                                           ).then_inc(drained[u.bank], 1)
                    if j == 3:
                        if S.runs("E"):
                            square(S, "E", 1)
                        if S.runs("P"):
                            high_half(S, "P", "norm2", pair2, hi2_ready)
                    if j == 4:
                        if S.runs("P"):
                            for h in range(2):
                                u = use(S, "router", h)
                                act.wait_ge(filled, u.filled())
                                act.activation(routed[:, h * HALF:(h + 1) * HALF],
                                               work[u.bank][0:2 * RH, 0:HALF], ACT.Relu
                                               ).then_inc(routed_hi, 1)
                        if S.runs("E"):
                            high_half(S, "E", "norm1", pair1, hi1_ready)
                    if j == 5:
                        if S.runs("E"):
                            for h in range(2):
                                u = use(S, "query", h)
                                act.wait_ge(filled, u.filled())
                                act.activation(query_hi[:, S.ring("E"), h * HALF:(h + 1) * HALF],
                                               work[u.bank][:, 0:HALF], ACT.Copy
                                               ).then_inc(drained[u.bank], 1)
                    if j == 6:
                        if S.runs("A"):
                            for h in range(2):
                                u = use(S, "shifted", h)
                                act.wait_ge(filled, u.filled())
                                act.activation(shifted[0][:, S.ring("A"), h * HALF:(h + 1) * HALF],
                                               work[u.bank][:, 0:HALF], ACT.Copy).then_inc(shifted_hi, 1)
                        if S.runs("P"):
                            act.wait_ge(route_step, S.count("P", ROUTE, EXPO_AT))
                            act.activation(expo[:, :, :], expo[:, :, :], ACT.Exp).then_inc(expo_ready, 1)
                            act.wait_ge(route_step, S.count("P", ROUTE, GAP_AT))
                            act.activation(gap_exp[:, :], gap[:, :], ACT.Exp).then_inc(gap_ready, 1)
                        if S.runs("B"):
                            for h in range(2):
                                act.wait_ge(attended, S.count("B", 2 * NT, 2 * NT - 1 + h))
                                act.activation(attn_t[:, h * HALF:(h + 1) * HALF],
                                               ps_attn[0:D + 1, h, 0:HALF], ACT.Copy
                                               ).then_inc(attn_copied, 1)
                        if S.runs("P"):
                            for h in range(2):
                                u = use(S, "weights", h)
                                act.wait_ge(filled, u.filled())
                                act.activation(weights_t[:, S.ring("P"), h * HALF:(h + 1) * HALF],
                                               work[u.bank][0:4 * E_, 0:HALF], ACT.Copy
                                               ).then_inc(drained[u.bank], 1)

            def square(S, stage, k):
                act.wait_ge(norm_step[k], S.count(stage, 6, 2))
                if S.has(stage, 1):
                    act.wait_ge(squares_ready[k], S.count(stage, 1, back=1))
                act.activation(sq[k][:, :], xc[k][:, :], ACT.Square).then_inc(sq_ready[k], 1)

            def high_half(S, stage, name, pair, hi_ready):
                for h in range(2):
                    u = use(S, name, h)
                    act.wait_ge(filled, u.filled())
                    act.activation(pair[:, S.ring(stage), h * HALF:(h + 1) * HALF],
                                   work[u.bank][:, 0:HALF], ACT.Copy, bias=1.0 / D).then_inc(hi_ready, 1)

            run_steps(act, body)

        @block.vector
        def _(dve):
            made = 0

            def prep(instruction):
                nonlocal made
                made += 1
                instruction.then_inc(prep_copied, 1)

            dve.wait_ge(weights_loaded, 16 * N_LOADS)
            dve.wait_ge(consts_made, N_CONSTS)
            dve.wait_ge(prep_filled, 1)
            prep(dve.tensor_copy(query_t[:, :], ps_moe[0:D, P:2 * P]))
            prep(dve.tensor_copy(key_t[:, :], ps_moe[0:D, 2 * P:3 * P]))
            for k in range(2):
                r = slice(k * D, (k + 1) * D)
                prep(dve.tensor_copy(embed_w[r, r], ps_moe[r, 0:D]))
            for i, (c, n) in enumerate(((0, EC), (EC, NF - EC))):
                prep(dve.tensor_copy(first_w[0][:, c:c + n], ps_attn[:, i, 0:n]))
                dve.wait_ge(prep_copied, made)
                prep(dve.tensor_tensor(first_w[1][:, c:c + n], ps_attn[:, i, 0:n],
                                       first_w[0][:, c:c + n].bitcast(F32), ALU.subtract))
            dve.wait_ge(prep_filled, 2)
            prep(dve.tensor_copy(score_w[0][:, :], work[0][:, 0:P]))
            dve.wait_ge(prep_copied, made)
            prep(dve.tensor_tensor(score_w[1][:, :], work[0][:, 0:P], score_w[0][:, :].bitcast(F32),
                                   ALU.subtract))
            prep(dve.tensor_copy(router2[:, 0:E_], raw_r2[:, :]))
            prep(dve.tensor_copy(b3_hi[:, :], raw_b3[:, :]))
            prep(dve.tensor_scalar(is_lo_row[:, :], is_hi_row[:, :], -1.0, 1.0, ALU.mult, ALU.add))
            prep(dve.tensor_copy(pick[:, :], raw_pick[:, :, :, :].rearrange("p q k d -> p (q k d)")))
            prep(dve.tensor_scalar(ones_r[:, :], ident[:, :], 0.0, 1.0, ALU.mult, ALU.add))
            dve.wait_ge(prep_copied, made)
            prep(dve.tensor_tensor(router2[:, E_:2 * E_], raw_r2[:, :], router2[:, 0:E_].bitcast(F32),
                                   ALU.subtract))
            prep(dve.tensor_tensor(b3_lo[:, :], raw_b3[:, :], b3_hi[:, :].bitcast(F32), ALU.subtract))
            dve.wait_ge(prep_copied, made)
            prep(dve.tensor_tensor(b3_low_rows[:, :], b3_lo[:, :], is_lo_row[:, :], ALU.mult))
            prep(dve.tensor_tensor(raw_b3[:, :], b3_hi[:, :].bitcast(F32), is_hi_row[:, :], ALU.mult))
            dve.wait_ge(prep_copied, made)
            prep(dve.tensor_tensor(b3[:, :], raw_b3[:, :], b3_low_rows[:, :], ALU.add))
            assert made == N_PREP

            def low_half(S, stage, name, pair, hi_ready):
                for h in range(2):
                    u = use(S, name, h)
                    cols = slice(h * HALF, (h + 1) * HALF)
                    dve.wait_ge(hi_ready, S.count(stage, 2, h + 1))
                    dve.scalar_tensor_tensor(out=pair[D:P, S.ring(stage), cols], in0=work[u.bank][D:P, 0:HALF],
                                             scalar=1.0 / D, in1=pair[D:P, S.ring(stage), cols].bitcast(F32),
                                             op0=ALU.add, op1=ALU.subtract
                                             ).then_inc(drained[u.bank], 1)

            def sum_tokens(S, stage, k, src):
                if S.has(stage, 1):
                    dve.wait_ge(norm_step[k], S.count(stage, 6, 1, back=1))
                dve.tensor_reduce(stat[k][0][:, :], groups(src), AX.X, ALU.add).then_inc(total_ready[k], 1)

            def sum_squares(S, stage, k):
                dve.wait_ge(sq_ready[k], S.count(stage, 1))
                if S.has(stage, 1):
                    dve.wait_ge(norm_step[k], S.count(stage, 6, 3, back=1))
                dve.tensor_reduce(stat[k][2][:, :], groups(sq[k][:, :]), AX.X, ALU.add
                                  ).then_inc(squares_ready[k], 1)

            routed_steps = 0

            def route_from(k):
                nonlocal routed_steps
                routed_steps = k

            def step_done(S, instruction):
                nonlocal routed_steps
                routed_steps += 1
                instruction.then_inc(route_step, 1)
                dve.wait_ge(route_step, S.count("P", ROUTE, routed_steps))

            def choose(S):
                def done(instruction):
                    step_done(S, instruction)

                route_from(0)
                u = use(S, "logits")
                dve.wait_ge(filled, u.filled())
                logits = work[u.bank][0:ROWS, 0:2 * E_ * G].rearrange("p (g e) -> p g e", e=2 * E_)
                many = [ROWS, G, E_]
                prios = prio[0:ROWS, :].unsqueeze(1).broadcast_to(many)
                done(dve.tensor_tensor(lg_hi[:, :, :], logits[:, :, 0:E_],
                                       router_bias[:, :].unsqueeze(1).broadcast_to(many), ALU.add))
                dve.tensor_tensor(lg[:, :, :], lg_hi[:, :, :], logits[:, :, E_:2 * E_], ALU.add
                                  ).then_inc(drained[u.bank], 1)
                wait_read(dve, u)
                for n, left in enumerate((lg, lg_rest)):
                    done(dve.tensor_reduce(best[:, n, :], left[:, :, :], AX.X, ALU.max))
                    done(dve.tensor_tensor(tie[:, :, :], left[:, :, :], wide(best[:, n, :], E_), ALU.is_equal))
                    done(dve.tensor_tensor(tie[:, :, :], tie[:, :, :], prios, ALU.mult))
                    done(dve.tensor_reduce(first_tie[:, :], tie[:, :, :], AX.X, ALU.max))
                    done(dve.tensor_tensor(chosen[:, n, :, :], tie[:, :, :], wide(first_tie[:, :], E_),
                                           ALU.is_equal))
                    if n == 0:
                        done(dve.scalar_tensor_tensor(out=lg_rest[:, :, :], in0=chosen[:, 0, :, :],
                                                      scalar=-BIG, in1=lg[:, :, :],
                                                      op0=ALU.mult, op1=ALU.add))
                done(dve.tensor_tensor(expo[:, :, 0:E_], lg[:, :, :], wide(best[:, 0, :], E_), ALU.subtract))
                done(dve.tensor_tensor(expo[:, :, E_], best[:, 1, :], best[:, 0, :], ALU.subtract))
                assert routed_steps == EXPO_AT

            def weigh(S):
                def done(instruction):
                    step_done(S, instruction)

                route_from(EXPO_AT)
                dve.wait_ge(expo_ready, S.count("P", 1))
                done(dve.tensor_reduce(expo_sum[:, :], expo[:, :, 0:E_], AX.X, ALU.add))
                done(dve.reciprocal(expo_inv[:, :], expo_sum[:, :]))
                done(dve.scalar_tensor_tensor(out=gap[:, :], in0=expo[:, :, E_], scalar=1.0,
                                              in1=expo_inv[:, :], op0=ALU.subtract, op1=ALU.mult))
                assert routed_steps == GAP_AT
                dve.wait_ge(gap_ready, S.count("P", 1))
                done(dve.tensor_scalar(gap[:, :], gap_exp[:, :], 1.0, None, ALU.add))
                done(dve.reciprocal(share[:, 0, :], gap[:, :]))
                done(dve.tensor_tensor(share[:, 1, :], gap_exp[:, :], share[:, 0, :], ALU.mult))
                done(dve.tensor_tensor(wsum[:, :, :, :], chosen[:, :, :, :],
                                       share[:, :, :].unsqueeze(3).broadcast_to([ROWS, 2, G, E_]), ALU.mult))
                done(dve.tensor_tensor(wts[:, :, :], wsum[:, 0, :, :], wsum[:, 1, :, :], ALU.add))
                done(dve.tensor_copy(wts_hi[:, :, :], wts[:, :, :]))
                both = [ROWS, G, 2, E_]
                pairs = wts_pair[:, :, :].rearrange("p g (k e) -> p g k e", k=2)
                high = wts_hi[:, :, :].bitcast(F32).unsqueeze(2).broadcast_to(both)
                done(dve.tensor_copy(pairs[:, :, :, 0:E_], high))
                done(dve.tensor_tensor(pairs[:, :, :, E_:2 * E_], wts[:, :, :].unsqueeze(2).broadcast_to(both),
                                       high, ALU.subtract))
                assert routed_steps == ROUTE

            def body(S):
                for j in range(NT):
                    if j < CHUNKS and S.runs("F"):
                        u = use(S, "spread", j)
                        dve.wait_ge(filled, u.filled())
                        wait_read(dve, use(S, "hidden2", j))
                        dve.tensor_tensor(scaled[:, j % 2, :], act2[:, j % 2, :], work[u.bank][:, 0:HALF],
                                          ALU.mult).then_inc(drained[u.bank], 1)
                    if S.runs("A"):
                        for t in score_tiles(j):
                            n = width(t)
                            for h in range(2):
                                u = use(S, "scores", t, h)
                                dve.wait_ge(filled, u.filled())
                                dve.tensor_reduce(row_max[0:n, t, h:h + 1], work[u.bank][0:n, 0:HALF],
                                                  AX.X, ALU.max).then_inc(drained[u.bank], 1)
                            for h in range(2):
                                wait_read(dve, use(S, "scores", t, h))
                            if S.has("A", 1):
                                dve.wait_ge(diag_ready, S.count("A", NT, t + 1, back=1))
                            dve.tensor_reduce(minus_max[0:n, t:t + 1], row_max[0:n, t, :], AX.X, ALU.max,
                                              negate=True).then_inc(max_ready, 1)
                    if j == 0 and S.runs("P"):
                        for i in range(2):
                            u = use(S, "attn", i)
                            gs = slice(i * (G // 2), (i + 1) * (G // 2))
                            src = work[u.bank][0:ROWS, 0:(G // 2) * (D + 1)].rearrange(
                                "p (g d) -> p g d", d=D + 1)
                            dve.wait_ge(filled, u.filled())
                            dve.reciprocal(inv_sum[:, gs], src[:, :, D]).then_inc(sums_inverted, 1)
                            dve.wait_ge(sums_inverted, S.count("P", 2, i + 1))
                            if S.has("P", 1):
                                dve.wait_ge(h2_ready, S.count("P", 1, back=1))
                            dve.tensor_tensor(groups(attn[:, :])[:, gs, :], src[:, :, 0:D],
                                              wide(inv_sum[:, :])[:, gs, :], ALU.mult
                                              ).then_inc(drained[u.bank], 1)
                    if j == 1 and S.runs("X"):
                        k = S.ring("X")
                        dve.wait_ge(pixels_loaded[k], 2 * S.ring_dma("X"))
                        if S.has("X", 1):
                            dve.wait_ge(patches_ready, S.count("X", 1, back=1))
                        dve.tensor_copy(by_patch[:, :].rearrange("r (w p q) -> r p w q", p=PATCH, q=PATCH),
                                        pixels[:, k, :].rearrange("r (p w q) -> r p w q", p=PATCH, q=PATCH)
                                        ).then_inc(by_patch_ready, 1)
                    if j == 1 and S.runs("P"):
                        dve.wait_ge(h2_ready, S.count("P", 1))
                        sum_tokens(S, "P", 2, h2[:, S.ring("P"), :])
                    if j == 2:
                        if S.runs("E"):
                            wait_read(dve, use(S, "tokens"))
                            sum_tokens(S, "E", 1, h1[:, S.ring("E"), :])
                        if S.runs("P"):
                            sum_squares(S, "P", 2)
                    if j == 3:
                        if S.runs("E"):
                            sum_squares(S, "E", 1)
                        if S.runs("P"):
                            low_half(S, "P", "norm2", pair2, hi2_ready)
                    if j == 4:
                        if S.runs("P"):
                            for h in range(2):
                                u = use(S, "router", h)
                                cols = slice(h * HALF, (h + 1) * HALF)
                                dve.wait_ge(routed_hi, S.count("P", 2, h + 1))
                                dve.scalar_tensor_tensor(out=routed[RH:2 * RH, cols],
                                                         in0=work[u.bank][RH:2 * RH, 0:HALF], scalar=0.0,
                                                         in1=routed[RH:2 * RH, cols].bitcast(F32),
                                                         op0=ALU.max, op1=ALU.subtract
                                                         ).then_inc(drained[u.bank], 1)
                        if S.runs("E"):
                            low_half(S, "E", "norm1", pair1, hi1_ready)
                    if j == 5 and S.runs("P"):
                        choose(S)
                    if j == 6:
                        if S.runs("A"):
                            for h in range(2):
                                u = use(S, "shifted", h)
                                cols = slice(h * HALF, (h + 1) * HALF)
                                k = S.ring("A")
                                dve.wait_ge(shifted_hi, S.count("A", 2, h + 1))
                                dve.tensor_tensor(shifted[1][:, k, cols], work[u.bank][:, 0:HALF],
                                                  shifted[0][:, k, cols].bitcast(F32), ALU.subtract
                                                  ).then_inc(drained[u.bank], 1)
                        if S.runs("P"):
                            weigh(S)
                        if S.runs("E"):
                            u = use(S, "values")
                            k = S.ring("E")
                            full = NT - 1
                            n = width(full)
                            dve.wait_ge(filled, u.filled())
                            dve.tensor_copy(values[:, k, 0:full, 0:D],
                                            work[u.bank][:, 0:full * D].rearrange("p (t d) -> p t d", d=D))
                            dve.tensor_copy(values[0:n, k, full, 0:D], work[u.bank][0:n, full * D:NT * D]
                                            ).then_inc(drained[u.bank], 1)
                        if S.runs("F"):
                            u = use(S, "back")
                            k = S.ring("F")
                            dve.wait_ge(filled, u.filled())
                            if S.has("F", RING):
                                dve.wait_ge(stored[k], S.ring_dma("F", back=RING))
                            dve.tensor_tensor(result[:, k, :], work[u.bank][0:ROWS, :], h2[:, k, :], ALU.add
                                              ).then_inc(drained[u.bank], 1)

            run_steps(dve, body)

    return nc


_INS = ["x", "txt", "L0_tok_W", "L0_tok_b", "L0_attn_Wq", "L0_attn_bq", "L0_attn_Wk", "L0_attn_bk",
        "L0_attn_Wv", "L0_attn_bv", "L0_ffn_router_w1", "L0_ffn_router_b1", "L0_ffn_router_w2",
        "L0_ffn_router_b2", "L0_ffn_expert_w1", "L0_ffn_expert_b1", "L0_ffn_expert_w2",
        "L0_ffn_expert_b2", "L0_ffn_expert_w3", "L0_ffn_expert_b3"]


def kernel(**inputs):
    import numpy as np
    import concourse.bacc as bacc
    from concourse.bass_utils import run_bass_kernel_spmd

    nc = bacc.Bacc("TRN2", target_bir_lowering=False, num_devices=1)
    arrays, args = {}, []
    for name in _INS:
        a = np.ascontiguousarray(inputs[name])
        arrays[f"in_{name}"] = a
        args.append(nc.dram_tensor(f"in_{name}", a.shape, mybir.dt.from_np(a.dtype), kind="ExternalInput").ap())
    out = nc.dram_tensor("out", (BATCH, TOK, D), F32, kind="ExternalOutput").ap()
    encoder_kernel(nc, *args, out)
    r = run_bass_kernel_spmd(nc, [arrays], core_ids=[0])
    return r.results[0]["out"]
```

```python
from contextlib import ExitStack

import concourse.bass as bass
from concourse import mybir

F32 = mybir.dt.float32
F32R = mybir.dt.float32r
ALU = mybir.AluOpType
ACT = mybir.ActivationFunctionType
AX = mybir.AxisListType

P = 128
BATCH = 32
D = 64
IMG = 224
PATCH = 8
SIDE = IMG // PATCH
WP2 = SIDE // 4
HROW = IMG // 2
TXT = 32
NIMG = SIDE * SIDE // 2
TOK = SIDE * SIDE + TXT
HALF = TOK // 2
ROWS = 102
TT = HALF // ROWS
G = 2 * TT
NT = -(-TOK // P)
E_ = 6
RH = 32
PAIRS = E_ // 2
CHUNKS = 2 * PAIRS
EPS = 1e-5
SCALE = D ** -0.5
BIG = 3.0e38
RING = 3
LAG = dict(X=0, E=1, A=2, B=3, P=4, T=5, F=6)
DEPTH = max(LAG.values())
WORK = 5


def width(t):
    return min(P, TOK - P * t)


def score_tiles(j):
    return ((0,), (1,), (2,), (3,), (4, 5), (6,), ())[j]


def bank_users(j):
    out = []
    if j == 0:
        out += [("F", "hidden1", 0)]
    out += [("B", "scores_t", j, 0), ("B", "scores_t", j, 1)]
    if j < CHUNKS:
        out += [("F", "spread", j), ("F", "hidden2", j)]
    if j + 1 < CHUNKS:
        out += [("F", "hidden1", j + 1)]
    if j == 0:
        out += [("E", "embed"), ("P", "attn", 0), ("P", "attn", 1)]
    out += [("A", "scores", t, h) for t in score_tiles(j) for h in (0, 1)]
    out += {
        0: [],
        1: [("E", "tokens"), ("T", "router", 0), ("T", "router", 1)],
        2: [("X", "patches"), ("T", "logits")],
        3: [("A", "values")],
        4: [],
        5: [("E", "norm1", 0), ("E", "norm1", 1), ("P", "norm2", 0), ("P", "norm2", 1)],
        6: [("E", "query", 0), ("E", "query", 1), ("A", "shifted", 0), ("A", "shifted", 1), ("T", "weights", 0), ("T", "weights", 1),
            ("F", "back")],
    }[j]
    return out


class Use:

    def __init__(self, bank, filled, drained, step):
        self.bank, self.filled_at, self.drained_at, self.step = bank, filled, drained, step

    def filled(self):
        return self.filled_at + self.step.turn * self.step.filled_per_turn

    def drained(self):
        return self.drained_at + self.step.turn * self.step.drained_per_turn[self.bank]

    def read(self):
        return self.drained() + 1


class Step:

    def __init__(self, at, turn=0):
        self.at, self.turn = at, turn

    def runs(self, stage):
        return 0 <= self.at - LAG[stage] < BATCH

    def ring(self, stage):
        return (self.at - LAG[stage]) % RING

    def image(self, stage):
        return self.at - LAG[stage] + RING * self.turn

    def has(self, stage, back):
        return self.at - LAG[stage] - back >= 0

    def count(self, stage, each, part=None, back=0):
        b = self.at - LAG[stage] - back
        return b * each + (each if part is None else part) + self.turn * (RING * each)

    def ring_dma(self, stage, back=0):
        return 16 * ((self.at - LAG[stage] - back) // RING + 1) + self.turn * 16


FIRST_LOOPED = DEPTH + 1
TURNS = (BATCH - FIRST_LOOPED) // RING
AFTER_LOOP = FIRST_LOOPED + TURNS * RING
LAST = BATCH + DEPTH


def plan():
    uses, filled, drained = {}, 0, [0] * WORK
    in_step = [name for j in range(NT) for name in bank_users(j)]

    def walk(steps):
        nonlocal filled
        for s in steps:
            at = (s - FIRST_LOOPED) % RING * len(in_step)
            for n, (stage, *name) in enumerate(in_step):
                if Step(s).runs(stage):
                    bank = (at + n) % WORK
                    uses[s, tuple(name)] = (bank, filled + 1, drained[bank])
                    filled += 1
                    drained[bank] += 1

    walk(range(FIRST_LOOPED))
    before, were = filled, list(drained)
    walk(range(FIRST_LOOPED, FIRST_LOOPED + RING))
    per_turn = filled - before
    drained_per_turn = [a - b for a, b in zip(drained, were)]
    filled += (TURNS - 1) * per_turn
    for k in range(WORK):
        drained[k] += (TURNS - 1) * drained_per_turn[k]
    walk(range(AFTER_LOOP, LAST))
    return uses, per_turn, drained_per_turn


USES, FILLED_PER_TURN, DRAINED_PER_TURN = plan()
Step.filled_per_turn = FILLED_PER_TURN
Step.drained_per_turn = DRAINED_PER_TURN


def use(step, *name):
    return Use(*USES[step.at, name], step)


def last_use(step, *name):
    if step.at != AFTER_LOOP and step.at != FIRST_LOOPED:
        return Use(*USES[step.at - 1, name], step)
    turns = 1 if step.at == FIRST_LOOPED else 1 - TURNS
    at = FIRST_LOOPED + RING - 1
    bank, filled, drained = USES[at, name]
    return Use(bank, filled - turns * FILLED_PER_TURN, drained - turns * DRAINED_PER_TURN[bank], step)


for _name in (("query", 1), ("shifted", 1), ("weights", 1), ("norm2", 1), ("values",)):
    _u = last_use(Step(FIRST_LOOPED), *_name)
    assert (_u.bank, _u.filled_at, _u.drained_at) == USES[FIRST_LOOPED - 1, _name]


def run_steps(eng, body):
    for s in range(FIRST_LOOPED):
        body(Step(s))
    with eng.Fori(0, TURNS) as turn:
        for u in range(RING):
            body(Step(FIRST_LOOPED + u, turn))
    for s in range(AFTER_LOOP, LAST):
        body(Step(s))


def encoder_kernel(nc, x, txt, tok_W, tok_b, Wq, bq, Wk, bk, Wv, bv, r_w1, r_b1, r_w2, r_b2,
                   e_w1, e_b1, e_w2, e_b2, e_w3, e_b3, out):
    ctx = ExitStack()
    with ctx:
        def sb(name, shape, dt=F32):
            return ctx.enter_context(nc.sbuf_tensor(name, shape, dt))

        def sem(name):
            return ctx.enter_context(nc.semaphore(name))

        work = [ctx.enter_context(nc.psum_tensor(f"work{k}", [P, 512], F32)) for k in range(WORK)]
        ps_attn = ctx.enter_context(nc.psum_tensor("ps_attn", [P, 2, 512], F32))
        ps_moe = ctx.enter_context(nc.psum_tensor("ps_moe", [P, 512], F32))

        ident = sb("ident", [P, P])
        ones_r = sb("ones_r", [P, P], F32R)
        center = sb("center", [D + 1, 2 * D])
        prio = sb("prio", [P, E_])
        minus_half = sb("minus_half", [P, G])
        one_of_d = sb("one_of_d", [P, G])
        raw_tok = sb("raw_tok", [D, 2 * D])
        tok_bias = sb("tok_bias", [P, 1])
        embed_w = sb("embed_w", [P, P])
        NF = 2 * D + 2 * RH + E_ * D
        QC, VC, RC, EC = 0, D, 2 * D, 2 * D + 2 * RH
        raw_first = sb("raw_first", [D + 1, NF])
        raw_k = sb("raw_k", [D + 1, D])
        query_t = sb("query_t", [D, 2 * D])
        key_t = sb("key_t", [D, 2 * D])
        score_w = [sb("score_w_hi", [P, P], F32R), sb("score_w_lo", [P, P], F32R)]
        first_w = [sb("first_w_hi", [P, NF], F32R), sb("first_w_lo", [P, NF], F32R)]
        w2 = sb("w2", [P, PAIRS, P])
        b2 = sb("b2", [P, PAIRS])
        w3 = sb("w3", [P, PAIRS, D])
        raw_r2 = sb("raw_r2", [2 * RH, E_])
        router2 = sb("router2", [2 * RH, 2 * E_], F32R)
        router_bias = sb("router_bias", [ROWS, E_])
        raw_b3 = sb("raw_b3", [4 * E_, D])
        b3_hi = sb("b3_hi", [4 * E_, D], F32R)
        b3_lo = sb("b3_lo", [4 * E_, D])
        b3_low_rows = sb("b3_low_rows", [4 * E_, D])
        is_hi_row = sb("is_hi_row", [4 * E_, D])
        is_lo_row = sb("is_lo_row", [4 * E_, D])
        b3 = sb("b3", [4 * E_, D], F32R)
        raw_pick = sb("raw_pick", [4 * E_, PAIRS, 2, D])
        pick = sb("pick", [4 * E_, PAIRS * P], F32R)

        pixels = sb("pixels", [2 * SIDE, RING, PATCH * HROW])
        by_patch = sb("by_patch", [2 * SIDE, PATCH * HROW])
        text = sb("text", [TXT // 2, RING, 2 * D])
        patches = sb("patches", [P, NIMG])
        embed_t = sb("embed_t", [P, HALF])
        h1 = sb("h1", [ROWS, RING, G * D])
        stat = {k: [sb(f"{n}{k}", [ROWS, G]) for n in ("total", "mean", "squares", "var", "rstd")]
                for k in (1, 2)}
        xc = {k: sb(f"xc{k}", [ROWS, G * D]) for k in (1, 2)}
        sq = {k: sb(f"sq{k}", [ROWS, G * D]) for k in (1, 2)}
        xn = {k: sb(f"xn{k}", [ROWS, G, 2 * D]) for k in (1, 2)}
        pair1 = sb("pair1", [P, RING, TOK], F32R)
        pair2 = sb("pair2", [P, RING, TOK], F32R)
        query_hi = sb("query_hi", [P, RING, TOK], F32R)
        values = sb("values", [P, RING, NT, D + 1])
        row_max = sb("row_max", [P, NT, 2])
        minus_max = sb("minus_max", [P, NT])
        max_diag = sb("max_diag", [P, TOK], F32R)
        shifted = [sb("shifted_hi", [P, RING, TOK], F32R), sb("shifted_lo", [P, RING, TOK], F32R)]
        probs = sb("probs", [P, 3, TOK])
        attn_t = sb("attn_t", [D + 1, TOK])
        inv_sum = sb("inv_sum", [ROWS, G])
        attn = sb("attn", [ROWS, G * D])
        h2 = sb("h2", [ROWS, RING, G * D])
        routed = sb("routed", [2 * RH, TOK], F32R)
        lg = sb("lg", [ROWS, G, E_])
        lg_hi = sb("lg_hi", [ROWS, G, E_])
        lg_rest = sb("lg_rest", [ROWS, G, E_])
        best = sb("best", [ROWS, 2, G])
        tie = sb("tie", [ROWS, G, E_])
        first_tie = sb("first_tie", [ROWS, G])
        chosen = sb("chosen", [ROWS, 2, G, E_])
        expo = sb("expo", [ROWS, G, E_ + 1])
        expo_sum = sb("expo_sum", [ROWS, G])
        expo_inv = sb("expo_inv", [ROWS, G])
        gap = sb("gap", [ROWS, G])
        gap_exp = sb("gap_exp", [ROWS, G])
        share = sb("share", [ROWS, 2, G])
        wsum = sb("wsum", [ROWS, 2, G, E_])
        wts = sb("wts", [ROWS, G, E_])
        wts_hi = sb("wts_hi", [ROWS, G, E_], F32R)
        wts_pair = sb("wts_pair", [ROWS, G, 4 * E_])
        weights_t = sb("weights_t", [4 * E_, RING, TOK], F32R)
        act1 = sb("act1", [P, 2, HALF])
        act2 = sb("act2", [P, 2, HALF])
        scaled = sb("scaled", [P, 2, HALF])
        moe_t = sb("moe_t", [D, TOK])
        result = sb("result", [ROWS, RING, G * D])

        tok_loaded = sem("tok_loaded")
        weights_loaded = sem("weights_loaded")
        consts_made = sem("consts_made")
        prep_filled = sem("prep_filled")
        prep_copied = sem("prep_copied")
        pixels_loaded = [sem(f"pixels_loaded{k}") for k in range(RING)]
        text_loaded = [sem(f"text_loaded{k}") for k in range(RING)]
        stored = [sem(f"stored{k}") for k in range(RING)]
        filled = sem("filled")
        drained = [sem(f"drained{k}") for k in range(WORK)]
        by_patch_ready = sem("by_patch_ready")
        patches_ready = sem("patches_ready")
        total_ready = {k: sem(f"total_ready{k}") for k in (1, 2)}
        norm_step = {k: sem(f"norm_step{k}") for k in (1, 2)}
        var_step = {k: sem(f"var_step{k}") for k in (1, 2)}
        hi1_ready = sem("hi1_ready")
        hi2_ready = sem("hi2_ready")
        max_ready = sem("max_ready")
        diag_ready = sem("diag_ready")
        shifted_hi = sem("shifted_hi")
        attended = sem("attended")
        attn_copied = sem("attn_copied")
        sums_inverted = sem("sums_inverted")
        h2_ready = sem("h2_ready")
        routed_hi = sem("routed_hi")
        route_step = sem("route_step")
        expo_ready = sem("expo_ready")
        gap_ready = sem("gap_ready")
        chunk_done = sem("chunk_done")
        moe_copied = sem("moe_copied")
        EXPO_AT, GAP_AT, WEIGHTS_AT, ROUTE = 14, 17, 22, 25
        PREPARE_AT = (1, 5)
        N_LOADS = 29
        N_CONSTS = 16 + E_
        N_PREP = 20

        block = ctx.enter_context(nc.Block())

        def groups(ap):
            return ap.rearrange("p (g d) -> p g d", d=D)

        def wide(stat_ap, n=D):
            return stat_ap.unsqueeze(2).broadcast_to([ROWS, G, n])

        def wait_read(eng, u):
            eng.wait_ge(drained[u.bank], u.read())

        @block.sync
        def _(sp):
            def load(dst, src):
                sp.dma_start(dst, src).then_inc(weights_loaded, 16)

            def load_image(S):
                if S.has("X", RING):
                    sp.wait_ge(by_patch_ready, S.count("X", 1, back=RING))
                    sp.wait_ge(patches_ready, S.count("X", 1, back=RING))
                b = S.image("X")
                k = S.ring("X")
                rows = x[b, 0].rearrange("(r p) w -> r p w", p=PATCH)
                for h in range(2):
                    sp.dma_start(pixels[h * SIDE:(h + 1) * SIDE, k, :].rearrange("r (p w) -> r p w", p=PATCH),
                                 rows[:, :, h * HROW:(h + 1) * HROW]).then_inc(pixels_loaded[k], 16)
                sp.dma_start(text[:, k, :], txt[b].rearrange("(r p) d -> r (p d)", p=2)
                             ).then_inc(text_loaded[k], 16)

            load_image(Step(0))
            for k in range(2):
                sp.dma_start(raw_tok[:, k * D:(k + 1) * D], tok_W).then_inc(tok_loaded, 16)
                sp.dma_start(tok_bias[k * D:(k + 1) * D, :], tok_b.rearrange("(d o) -> d o", o=1)
                             ).then_inc(tok_loaded, 16)
            for c, (w, b) in ((QC, (Wq, bq)), (VC, (Wv, bv)), (RC, (r_w1, r_b1)), (RC + RH, (r_w1, r_b1))):
                n = w.shape[1]
                load(raw_first[0:D, c:c + n], w)
                load(raw_first[D:D + 1, c:c + n], b.rearrange("(o d) -> o d", o=1))
            load(raw_first[0:D, EC:NF].rearrange("p (e h) -> p e h", e=E_), e_w1.rearrange("e d h -> d e h"))
            load(raw_first[D:D + 1, EC:NF], e_b1.rearrange("(o e) h -> o (e h)", o=1))
            load(raw_k[0:D, :], Wk)
            load(raw_k[D:D + 1, :], bk.rearrange("(o d) -> o d", o=1))
            sp.wait_ge(consts_made, 2)
            for k in range(2):
                load(w2[k * D:(k + 1) * D, :, k * D:(k + 1) * D],
                     e_w2.rearrange("(q k) h f -> k h q f", k=2)[k])
                for q in range(PAIRS):
                    load(b2[k * D:(k + 1) * D, q:q + 1], e_b2[2 * q + k].rearrange("(f o) -> f o", o=1))
                load(w3[k * D:(k + 1) * D, :, :], e_w3.rearrange("(q k) f o -> k f q o", k=2)[k])
                load(raw_r2[k * RH:(k + 1) * RH, :], r_w2)
            load(router_bias[:, :], r_b2.rearrange("(o e) -> o e", o=1).broadcast_to([ROWS, E_]))
            for k in range(4):
                load(raw_b3[k * E_:(k + 1) * E_, :], e_b3)

            def body(S):
                if S.runs("X") and S.at > 0:
                    load_image(S)
                if S.runs("F"):
                    b = S.image("F")
                    k = S.ring("F")
                    wait_read(sp, use(S, "back"))
                    sp.dma_start(out[b].rearrange("(t r p) d -> r t (p d)", t=TT, r=ROWS),
                                 result[:, k, :].rearrange("r (t q) -> r t q", t=TT)
                                 ).then_inc(stored[k], 16)

            run_steps(sp, body)
            for k in range(RING):
                sp.wait_ge(stored[k], 16 * len(range(k, BATCH, RING)))

        @block.gpsimd
        def _(pool):
            pool.memset(center[D:D + 1, :], 1.0).then_inc(consts_made, 1)
            pool.wait_ge(consts_made, 1)
            pool.memset(w2[:, :, :], 0.0).then_inc(consts_made, 1)
            pool.memset(embed_w[:, :], 0.0).then_inc(consts_made, 1)
            pool.memset(ident[:, :], 0.0).then_inc(consts_made, 1)
            pool.memset(center[0:D, :], -1.0 / D).then_inc(consts_made, 1)
            pool.memset(raw_pick[:, :, :, :], 0.0).then_inc(consts_made, 1)
            pool.memset(is_hi_row[:, :], 1.0).then_inc(consts_made, 1)
            pool.memset(minus_half[:, :], -0.5).then_inc(consts_made, 1)
            pool.memset(one_of_d[:, :], 1.0 / D).then_inc(consts_made, 1)
            for e in range(E_):
                pool.memset(prio[:, e:e + 1], float(E_ - e)).then_inc(consts_made, 1)
            pool.memset(values[:, :, :, :], 1.0).then_inc(consts_made, 1)
            pool.memset(max_diag[:, :].bitcast(F32), 0.0).then_inc(consts_made, 1)
            made = 11 + E_
            pool.wait_ge(consts_made, made)
            pool.affine_select(out=ident[:, :], in_=ident[:, :], compare_op=ALU.not_equal, fill=1.0,
                               base=0, pattern=[[-1, P]], channel_multiplier=1).then_inc(consts_made, 1)
            pool.affine_select(out=center[0:D, :].rearrange("p (k d) -> p k d", k=2),
                               in_=center[0:D, :].rearrange("p (k d) -> p k d", k=2),
                               compare_op=ALU.not_equal, fill=1.0 - 1.0 / D, base=0,
                               pattern=[[0, 2], [-1, D]], channel_multiplier=1).then_inc(consts_made, 1)
            pool.affine_select(out=is_hi_row[:, :], in_=is_hi_row[:, :], compare_op=ALU.is_ge, fill=0.0,
                               base=2 * E_ - 1, pattern=[[0, D]], channel_multiplier=-1
                               ).then_inc(consts_made, 1)
            for k in range(2):
                pool.affine_select(out=raw_pick[:, :, :, :], in_=raw_pick[:, :, :, :],
                                   compare_op=ALU.not_equal, fill=1.0, base=-E_ * k,
                                   pattern=[[-2, PAIRS], [-1, 2], [0, D]], channel_multiplier=1
                                   ).then_inc(consts_made, 1)
                pool.wait_ge(consts_made, made + 4 + k)

            def norm(S, stage, k, x_ap):
                step = norm_step[k]
                total, mean = stat[k][:2]
                pool.wait_ge(total_ready[k], S.count(stage, 1))
                if S.has(stage, 1):
                    pool.wait_ge(var_step[k], S.count(stage, 2, 1, back=1))
                pool.tensor_tensor(mean[:, :], total[:, :], one_of_d[0:ROWS, :], ALU.mult).then_inc(step, 1)
                pool.wait_ge(step, S.count(stage, 5, 1))
                pool.tensor_tensor(groups(xc[k][:, :]), groups(x_ap), wide(mean[:, :]), ALU.subtract
                                   ).then_inc(step, 1)
                pool.wait_ge(step, S.count(stage, 5, 2))
                pool.tensor_tensor(sq[k][:, :], xc[k][:, :], xc[k][:, :], ALU.mult).then_inc(step, 1)

            def norm_end(S, stage, k):
                step = norm_step[k]
                _, _, _, var, rstd = stat[k]
                pool.wait_ge(var_step[k], S.count(stage, 2))
                pool.tensor_tensor(rstd[:, :], var[:, :], minus_half[0:ROWS, :], ALU.pow).then_inc(step, 1)
                pool.wait_ge(step, S.count(stage, 5, 4))
                if S.has(stage, 1):
                    pool.wait_ge({1: hi1_ready, 2: hi2_ready}[k], S.count(stage, 2, back=1))
                both = [ROWS, G, 2, D]
                pool.tensor_tensor(xn[k][:, :, :].rearrange("p g (k d) -> p g k d", k=2),
                                   groups(xc[k][:, :]).unsqueeze(2).broadcast_to(both),
                                   rstd[:, :].unsqueeze(2).unsqueeze(3).broadcast_to(both), ALU.mult
                                   ).then_inc(step, 1)

            def body(S):
                for j in range(NT):
                    if S.runs("A"):
                        for t in score_tiles(j):
                            n = width(t)
                            pool.wait_ge(max_ready, S.count("A", NT, t + 1))
                            if t == 0 and S.has("A", 1):
                                pool.wait_ge(shifted_hi, S.count("A", 2, back=1))
                            pool.tensor_tensor(max_diag[0:n, t * P:t * P + n], ident[0:n, 0:n],
                                               minus_max[0:n, t:t + 1].broadcast_to([n, n]), ALU.mult
                                               ).then_inc(diag_ready, 1)
                    if j == 0 and S.runs("P"):
                        for i in range(2):
                            wait_read(pool, use(S, "attn", i))
                        pool.tensor_tensor(h2[:, S.ring("P"), :], attn[:, :], h1[:, S.ring("P"), :],
                                           ALU.add).then_inc(h2_ready, 1)
                    if j == 1 and S.runs("P"):
                        norm(S, "P", 2, h2[:, S.ring("P"), :])
                    if j == 2:
                        if S.runs("E"):
                            norm(S, "E", 1, h1[:, S.ring("E"), :])
                        if S.runs("P"):
                            norm_end(S, "P", 2)
                    if j == 3 and S.runs("E"):
                        norm_end(S, "E", 1)

            run_steps(pool, body)

        @block.tensor
        def _(pe):
            pe.wait_ge(consts_made, N_CONSTS)
            pe.wait_ge(tok_loaded, 16 * 4)
            pe.matmul(ps_moe[:, 0:D], raw_tok[:, :], ident[0:D, 0:D], start=True, stop=True
                      ).then_inc(prep_filled, 1)

            def prepare():
                pe.wait_ge(weights_loaded, 16 * N_LOADS)
                pe.matmul(ps_moe[0:D, P:2 * P], raw_first[:, QC:QC + D], center[:, :], start=True, stop=True)
                pe.matmul(ps_moe[0:D, 2 * P:3 * P], raw_k[:, :], center[:, :], start=True, stop=True)
                pe.matmul(ps_attn[:, 0, 0:EC], center[:, :], raw_first[:, 0:EC], start=True, stop=True)
                pe.matmul(ps_attn[:, 1, 0:NF - EC], center[:, :], raw_first[:, EC:NF], start=True, stop=True
                          ).then_inc(prep_filled, 1)
                pe.wait_ge(prep_copied, 4)
                pe.matmul(ps_moe[:, 3 * P:4 * P], query_t[:, :], key_t[:, :], start=True, stop=True
                          ).then_inc(prep_filled, 1)
                pe.wait_ge(prep_copied, N_PREP)

            def take(S, *name, after=()):
                u = use(S, *name)
                least = {u.bank: (u.drained_at, u.drained)} if u.drained_at > 0 else {}
                for v in after:
                    if v.drained_at + 1 > least.get(v.bank, (0,))[0]:
                        least[v.bank] = (v.drained_at + 1, v.read)
                for bank, (_, count) in least.items():
                    pe.wait_ge(drained[bank], count())
                return work[u.bank]

            def two_passes(dst, w, c, n, rhs):
                pe.matmul(dst, w[0][:, c:c + n], rhs, start=True, stop=False)
                return pe.matmul(dst, w[1][:, c:c + n], rhs, start=False, stop=True)

            def attend(S, t):
                n = width(t)
                for h in range(2):
                    wait_read(pe, use(S, "scores_t", t, h))
                    if t == 0 and S.has("B", 1):
                        pe.wait_ge(attn_copied, S.count("B", 2, h + 1, back=1))
                    pe.matmul(ps_attn[0:D + 1, h, 0:HALF], values[0:n, S.ring("B"), t, :],
                              probs[0:n, t % 3, h * HALF:(h + 1) * HALF],
                              start=(t == 0), stop=(t == NT - 1)).then_inc(attended, 1)

            def hidden1(S, c):
                h, q = divmod(c, PAIRS)
                bank = take(S, "hidden1", c)
                two_passes(bank[:, 0:HALF], first_w, EC + q * P, P,
                           pair2[:, S.ring("F"), h * HALF:(h + 1) * HALF]).then_inc(filled, 1)

            def experts_out(S, c):
                h, q = divmod(c, PAIRS)
                wait_read(pe, use(S, "spread", c))
                if q == 0 and (h == 1 or S.has("F", 1)):
                    pe.wait_ge(moe_copied, S.count("F", 2, h, back=0))
                pe.matmul(ps_moe[0:D, 0:HALF], w3[:, q, :], scaled[:, c % 2, :], start=(q == 0), stop=False)
                if q == PAIRS - 1:
                    pe.matmul(ps_moe[0:D, 0:HALF], b3[:, :],
                              weights_t[:, S.ring("F"), h * HALF:(h + 1) * HALF],
                              start=False, stop=True).then_inc(chunk_done, 1)

            def body(S):
                for j in range(NT):
                    if (S.at, j) == PREPARE_AT:
                        prepare()
                    h, q = divmod(j, PAIRS)
                    cols = slice(h * HALF, (h + 1) * HALF)
                    if j == 0 and S.runs("F"):
                        hidden1(S, 0)
                    if S.runs("B"):
                        n, k = width(j), S.ring("B")
                        for half in range(2):
                            bank = take(S, "scores_t", j, half,
                                        after=[last_use(S, "shifted", half), last_use(S, "values")]
                                        if j == 0 else [])
                            for part in range(2):
                                mm = pe.matmul(bank[0:n, 0:HALF], pair1[:, k, j * P:j * P + n],
                                               shifted[part][:, k, half * HALF:(half + 1) * HALF],
                                               start=(part == 0), stop=(part == 1))
                            mm.then_inc(filled, 1)
                    if j >= 1 and S.runs("F") and S.runs("B"):
                        experts_out(S, j - 1)
                    if j < CHUNKS and S.runs("F"):
                        bank = take(S, "spread", j, after=[last_use(S, "weights", h)])
                        pe.matmul(bank[:, 0:HALF], pick[:, q * P:(q + 1) * P],
                                  weights_t[:, S.ring("F"), cols], start=True, stop=True
                                  ).then_inc(filled, 1)
                        bank = take(S, "hidden2", j, after=[use(S, "hidden1", j)])
                        pe.matmul(bank[:, 0:HALF], w2[:, q, :], act1[:, j % 2, :], start=True, stop=True
                                  ).then_inc(filled, 1)
                    if j + 1 < CHUNKS and S.runs("F"):
                        hidden1(S, j + 1)
                    if j >= 1 and S.runs("F") and not S.runs("B"):
                        experts_out(S, j - 1)
                    if j >= 1 and S.runs("B"):
                        attend(S, j - 1)
                    if j == 0 and S.runs("E"):
                        pe.wait_ge(patches_ready, S.count("E", 1))
                        bank = take(S, "embed")
                        pe.matmul(bank[:, 0:NIMG], embed_w[:, :], patches[:, :], start=True, stop=True
                                  ).then_inc(filled, 1)
                    if j == 0 and S.runs("P"):
                        pe.wait_ge(attn_copied, S.count("P", 2))
                        for i in range(2):
                            bank = take(S, "attn", i)
                            for g in range(G // 2):
                                c = (i * (G // 2) + g) * ROWS
                                mm = pe.transpose(bank[0:ROWS, g * (D + 1):(g + 1) * (D + 1)],
                                                  attn_t[:, c:c + ROWS], ident[0:D + 1, 0:D + 1])
                            mm.then_inc(filled, 1)
                    if S.runs("A"):
                        k = S.ring("A")
                        for t in score_tiles(j):
                            n = width(t)
                            for h in range(2):
                                bank = take(S, "scores", t, h,
                                            after=[last_use(S, "query", 0), last_use(S, "query", 1)]
                                            if (t, h) == (0, 0) else [])
                                pe.matmul(bank[0:n, 0:HALF], query_hi[:, k, t * P:t * P + n],
                                          pair1[:, k, h * HALF:(h + 1) * HALF],
                                          start=True, stop=True).then_inc(filled, 1)
                    if j == 1 and S.runs("E"):
                        bank = take(S, "tokens", after=[use(S, "embed")])
                        for t in range(TT):
                            mm = pe.transpose(bank[0:ROWS, t * P:(t + 1) * P],
                                              embed_t[:, t * ROWS:(t + 1) * ROWS], ident[:, :])
                        mm.then_inc(filled, 1)
                    if j == 1 and S.runs("T"):
                        k = S.ring("T")
                        for h in range(2):
                            bank = take(S, "router", h, after=[last_use(S, "norm2", h)])
                            two_passes(bank[0:2 * RH, 0:HALF], first_w, RC, 2 * RH,
                                       pair2[:, k, h * HALF:(h + 1) * HALF]).then_inc(filled, 1)
                    if j == 2 and S.runs("X"):
                        k = S.ring("X")
                        pe.wait_ge(by_patch_ready, S.count("X", 1))
                        pe.wait_ge(text_loaded[k], S.ring_dma("X"))
                        bank = take(S, "patches")
                        n = 2 * SIDE
                        pe.matmul(bank[:, 0:n], by_patch[:, 0:P], ident[0:n, 0:n], start=True, stop=True)
                        for w in range(1, WP2):
                            pe.transpose(bank[:, w * n:(w + 1) * n], by_patch[:, w * P:(w + 1) * P],
                                         ident[0:n, 0:n])
                        pe.transpose(bank[:, NIMG:HALF], text[:, k, :], ident[0:TXT // 2, 0:TXT // 2]
                                     ).then_inc(filled, 1)
                    if j == 2 and S.runs("T"):
                        bank = take(S, "logits", after=[use(S, "router", 0), use(S, "router", 1)])
                        for g in range(G):
                            mm = pe.matmul(bank[0:ROWS, g * 2 * E_:(g + 1) * 2 * E_],
                                           routed[:, g * ROWS:(g + 1) * ROWS], router2[:, :],
                                           start=True, stop=True)
                        mm.then_inc(filled, 1)
                    if j == 3 and S.runs("A"):
                        k = S.ring("A")
                        bank = take(S, "values")
                        for t in range(NT):
                            n = width(t)
                            for part in range(2):
                                mm = pe.matmul(bank[0:n, t * D:(t + 1) * D],
                                               pair1[:, k, t * P:t * P + n],
                                               first_w[part][:, VC:VC + D],
                                               start=(part == 0), stop=(part == 1))
                        mm.then_inc(filled, 1)
                    if j == 5 and S.runs("E"):
                        pe.wait_ge(norm_step[1], S.count("E", 5))
                        turn_tokens(S, "norm1", xn[1])
                    if j == 5 and S.runs("P"):
                        pe.wait_ge(norm_step[2], S.count("P", 5))
                        turn_tokens(S, "norm2", xn[2])
                    if j == 6 and S.runs("E"):
                        k = S.ring("E")
                        for h in range(2):
                            bank = take(S, "query", h, after=[use(S, "norm1", h)])
                            two_passes(bank[:, 0:HALF], score_w, 0, P, pair1[:, k, h * HALF:(h + 1) * HALF]
                                       ).then_inc(filled, 1)
                    if j == 6:
                        if S.runs("A"):
                            k = S.ring("A")
                            pe.wait_ge(diag_ready, S.count("A", NT))
                            for h in range(2):
                                cols = slice(h * HALF, (h + 1) * HALF)
                                bank = take(S, "shifted", h)
                                for part in range(2):
                                    pe.matmul(bank[:, 0:HALF], score_w[part][:, :], pair1[:, k, cols],
                                              start=(part == 0), stop=False)
                                pe.matmul(bank[:, 0:HALF], ones_r[:, :], max_diag[:, cols],
                                          start=False, stop=True).then_inc(filled, 1)
                        if S.runs("B"):
                            attend(S, NT - 1)
                        if S.runs("T"):
                            pe.wait_ge(route_step, S.count("T", ROUTE))
                            for i in range(2):
                                bank = take(S, "weights", i)
                                for g in range(G // 2):
                                    mm = pe.transpose(bank[0:4 * E_, g * ROWS:(g + 1) * ROWS],
                                                      wts_pair[:, i * (G // 2) + g, :],
                                                      ident[0:ROWS, 0:ROWS])
                                mm.then_inc(filled, 1)
                        if S.runs("F"):
                            pe.wait_ge(moe_copied, S.count("F", 2))
                            bank = take(S, "back")
                            pe.matmul(bank[0:ROWS, 0:D], moe_t[:, 0:ROWS], ident[0:D, 0:D],
                                      start=True, stop=True)
                            for g in range(1, G):
                                mm = pe.transpose(bank[0:ROWS, g * D:(g + 1) * D],
                                                  moe_t[:, g * ROWS:(g + 1) * ROWS], ident[0:D, 0:D])
                            mm.then_inc(filled, 1)

            def turn_tokens(S, name, src):
                for i in range(2):
                    bank = take(S, name, i)
                    for g in range(G // 2):
                        mm = pe.transpose(bank[:, g * ROWS:(g + 1) * ROWS], src[:, i * (G // 2) + g, :],
                                          ident[0:ROWS, 0:ROWS])
                    mm.then_inc(filled, 1)

            run_steps(pe, body)

        @block.scalar
        def _(act):
            act.wait_ge(tok_loaded, 16 * 4)

            def body(S):
                for j in range(NT):
                    if (S.at, j) == PREPARE_AT:
                        act.wait_ge(weights_loaded, 16 * N_LOADS)
                    if j == 0 and S.runs("F"):
                        first_relu(S, 0)
                    if S.runs("B"):
                        n = width(j)
                        for h in range(2):
                            u = use(S, "scores_t", j, h)
                            act.wait_ge(filled, u.filled())
                            act.activation(probs[0:n, j % 3, h * HALF:(h + 1) * HALF],
                                           work[u.bank][0:n, 0:HALF], ACT.Exp, scale=SCALE
                                           ).then_inc(drained[u.bank], 1)
                    if S.runs("F"):
                        if j < CHUNKS:
                            u = use(S, "hidden2", j)
                            act.wait_ge(filled, u.filled())
                            act.activation(act2[:, j % 2, :], work[u.bank][:, 0:HALF], ACT.Relu,
                                           bias=b2[:, j % PAIRS:j % PAIRS + 1]
                                           ).then_inc(drained[u.bank], 1)
                        if j + 1 < CHUNKS:
                            first_relu(S, j + 1)
                        if j in (PAIRS, NT - 1):
                            h = 0 if j == PAIRS else 1
                            act.wait_ge(chunk_done, S.count("F", 2, h + 1))
                            act.activation(moe_t[:, h * HALF:(h + 1) * HALF], ps_moe[0:D, 0:HALF], ACT.Copy
                                           ).then_inc(moe_copied, 1)
                    if j == 4 and S.runs("T"):
                        act.wait_ge(route_step, S.count("T", ROUTE, EXPO_AT))
                        act.activation(expo[:, :, :], expo[:, :, :], ACT.Exp).then_inc(expo_ready, 1)
                    if j == 5 and S.runs("T"):
                        act.wait_ge(route_step, S.count("T", ROUTE, GAP_AT))
                        act.activation(gap_exp[:, :], gap[:, :], ACT.Exp).then_inc(gap_ready, 1)
                    if j == 0 and S.runs("E"):
                        u = use(S, "embed")
                        act.wait_ge(filled, u.filled())
                        act.activation(embed_t[:, 0:NIMG], work[u.bank][:, 0:NIMG], ACT.Identity,
                                       bias=tok_bias[:, :]).then_inc(drained[u.bank], 1)
                    if j == 1 and S.runs("E"):
                        u = use(S, "tokens")
                        act.wait_ge(filled, u.filled())
                        if S.has("E", RING):
                            act.wait_ge(h2_ready, S.count("E", 1, back=RING))
                        act.activation(h1[:, S.ring("E"), :], work[u.bank][0:ROWS, :], ACT.Copy
                                       ).then_inc(drained[u.bank], 1)
                    if j == 1 and S.runs("T"):
                        for h in range(2):
                            u = use(S, "router", h)
                            act.wait_ge(filled, u.filled())
                            act.activation(routed[:, h * HALF:(h + 1) * HALF],
                                           work[u.bank][0:2 * RH, 0:HALF], ACT.Relu
                                           ).then_inc(routed_hi, 1)
                    if j == 2:
                        if S.runs("X"):
                            u = use(S, "patches")
                            act.wait_ge(filled, u.filled())
                            act.activation(patches[:, :].rearrange("p (r h w) -> p w h r", h=2, w=WP2),
                                           work[u.bank][:, 0:NIMG].rearrange("p (w h r) -> p w h r", h=2, w=WP2),
                                           ACT.Copy).then_inc(patches_ready, 1)
                            act.activation(embed_t[:, NIMG:HALF], work[u.bank][:, NIMG:HALF], ACT.Copy
                                           ).then_inc(drained[u.bank], 1)
                    if j == 5:
                        if S.runs("E"):
                            high_half(S, "E", "norm1", pair1, hi1_ready)
                        if S.runs("P"):
                            high_half(S, "P", "norm2", pair2, hi2_ready)
                    if j == 6:
                        if S.runs("E"):
                            for h in range(2):
                                u = use(S, "query", h)
                                act.wait_ge(filled, u.filled())
                                act.activation(query_hi[:, S.ring("E"), h * HALF:(h + 1) * HALF],
                                               work[u.bank][:, 0:HALF], ACT.Copy
                                               ).then_inc(drained[u.bank], 1)
                    if j == 6:
                        if S.runs("A"):
                            for h in range(2):
                                u = use(S, "shifted", h)
                                act.wait_ge(filled, u.filled())
                                act.activation(shifted[0][:, S.ring("A"), h * HALF:(h + 1) * HALF],
                                               work[u.bank][:, 0:HALF], ACT.Copy).then_inc(shifted_hi, 1)
                        if S.runs("B"):
                            for h in range(2):
                                act.wait_ge(attended, S.count("B", 2 * NT, 2 * NT - 1 + h))
                                act.activation(attn_t[:, h * HALF:(h + 1) * HALF],
                                               ps_attn[0:D + 1, h, 0:HALF], ACT.Copy
                                               ).then_inc(attn_copied, 1)
                        if S.runs("T"):
                            for h in range(2):
                                u = use(S, "weights", h)
                                act.wait_ge(filled, u.filled())
                                act.activation(weights_t[:, S.ring("T"), h * HALF:(h + 1) * HALF],
                                               work[u.bank][0:4 * E_, 0:HALF], ACT.Copy
                                               ).then_inc(drained[u.bank], 1)

            def first_relu(S, c):
                u = use(S, "hidden1", c)
                act.wait_ge(filled, u.filled())
                act.activation(act1[:, c % 2, :], work[u.bank][:, 0:HALF], ACT.Relu
                               ).then_inc(drained[u.bank], 1)

            def high_half(S, stage, name, pair, hi_ready):
                for h in range(2):
                    u = use(S, name, h)
                    act.wait_ge(filled, u.filled())
                    act.activation(pair[:, S.ring(stage), h * HALF:(h + 1) * HALF],
                                   work[u.bank][:, 0:HALF], ACT.Copy, bias=1.0 / D).then_inc(hi_ready, 1)

            run_steps(act, body)

        @block.vector
        def _(dve):
            made = 0

            def prep(instruction):
                nonlocal made
                made += 1
                instruction.then_inc(prep_copied, 1)

            dve.wait_ge(consts_made, N_CONSTS)
            dve.wait_ge(prep_filled, 1)
            for k in range(2):
                r = slice(k * D, (k + 1) * D)
                prep(dve.tensor_copy(embed_w[r, r], ps_moe[r, 0:D]))

            def prepare():
                dve.wait_ge(weights_loaded, 16 * N_LOADS)
                dve.wait_ge(prep_filled, 2)
                prep(dve.tensor_copy(query_t[:, :], ps_moe[0:D, P:2 * P]))
                prep(dve.tensor_copy(key_t[:, :], ps_moe[0:D, 2 * P:3 * P]))
                for i, (c, n) in enumerate(((0, EC), (EC, NF - EC))):
                    prep(dve.tensor_copy(first_w[0][:, c:c + n], ps_attn[:, i, 0:n]))
                    dve.wait_ge(prep_copied, made)
                    prep(dve.tensor_tensor(first_w[1][:, c:c + n], ps_attn[:, i, 0:n],
                                           first_w[0][:, c:c + n].bitcast(F32), ALU.subtract))
                dve.wait_ge(prep_filled, 3)
                prep(dve.tensor_copy(score_w[0][:, :], ps_moe[:, 3 * P:4 * P]))
                dve.wait_ge(prep_copied, made)
                prep(dve.tensor_tensor(score_w[1][:, :], ps_moe[:, 3 * P:4 * P], score_w[0][:, :].bitcast(F32),
                                       ALU.subtract))
                prep(dve.tensor_copy(router2[:, 0:E_], raw_r2[:, :]))
                prep(dve.tensor_copy(b3_hi[:, :], raw_b3[:, :]))
                prep(dve.tensor_scalar(is_lo_row[:, :], is_hi_row[:, :], -1.0, 1.0, ALU.mult, ALU.add))
                prep(dve.tensor_copy(pick[:, :], raw_pick[:, :, :, :].rearrange("p q k d -> p (q k d)")))
                prep(dve.tensor_scalar(ones_r[:, :], ident[:, :], 0.0, 1.0, ALU.mult, ALU.add))
                dve.wait_ge(prep_copied, made)
                prep(dve.tensor_tensor(router2[:, E_:2 * E_], raw_r2[:, :], router2[:, 0:E_].bitcast(F32),
                                       ALU.subtract))
                prep(dve.tensor_tensor(b3_lo[:, :], raw_b3[:, :], b3_hi[:, :].bitcast(F32), ALU.subtract))
                dve.wait_ge(prep_copied, made)
                prep(dve.tensor_tensor(b3_low_rows[:, :], b3_lo[:, :], is_lo_row[:, :], ALU.mult))
                prep(dve.tensor_tensor(raw_b3[:, :], b3_hi[:, :].bitcast(F32), is_hi_row[:, :], ALU.mult))
                dve.wait_ge(prep_copied, made)
                prep(dve.tensor_tensor(b3[:, :], raw_b3[:, :], b3_low_rows[:, :], ALU.add))
                assert made == N_PREP

            def low_half(S, stage, name, pair, hi_ready):
                for h in range(2):
                    u = use(S, name, h)
                    cols = slice(h * HALF, (h + 1) * HALF)
                    dve.wait_ge(hi_ready, S.count(stage, 2, h + 1))
                    dve.scalar_tensor_tensor(out=pair[D:P, S.ring(stage), cols], in0=work[u.bank][D:P, 0:HALF],
                                             scalar=1.0 / D, in1=pair[D:P, S.ring(stage), cols].bitcast(F32),
                                             op0=ALU.add, op1=ALU.subtract
                                             ).then_inc(drained[u.bank], 1)

            def sum_tokens(S, stage, k, src):
                if S.has(stage, 1):
                    dve.wait_ge(norm_step[k], S.count(stage, 5, 1, back=1))
                dve.tensor_reduce(stat[k][0][:, :], groups(src), AX.X, ALU.add).then_inc(total_ready[k], 1)

            def variance(S, stage, k):
                _, _, squares, var, _ = stat[k]
                step = var_step[k]
                dve.wait_ge(norm_step[k], S.count(stage, 5, 3))
                dve.tensor_reduce(squares[:, :], groups(sq[k][:, :]), AX.X, ALU.add).then_inc(step, 1)
                dve.wait_ge(step, S.count(stage, 2, 1))
                dve.tensor_scalar(var[:, :], squares[:, :], 1.0 / D, EPS, ALU.mult, ALU.add).then_inc(step, 1)

            routed_steps = 0

            def route_from(k):
                nonlocal routed_steps
                routed_steps = k

            def step_done(S, instruction):
                nonlocal routed_steps
                routed_steps += 1
                instruction.then_inc(route_step, 1)
                dve.wait_ge(route_step, S.count("T", ROUTE, routed_steps))

            many = [ROWS, G, E_]

            def read_logits(S):
                def done(instruction):
                    step_done(S, instruction)

                route_from(0)
                u = use(S, "logits")
                dve.wait_ge(filled, u.filled())
                logits = work[u.bank][0:ROWS, 0:2 * E_ * G].rearrange("p (g e) -> p g e", e=2 * E_)
                done(dve.tensor_tensor(lg_hi[:, :, :], logits[:, :, 0:E_],
                                       router_bias[:, :].unsqueeze(1).broadcast_to(many), ALU.add))
                dve.tensor_tensor(lg[:, :, :], lg_hi[:, :, :], logits[:, :, E_:2 * E_], ALU.add
                                  ).then_inc(drained[u.bank], 1)

            def choose(S, n):
                def done(instruction):
                    step_done(S, instruction)

                left = (lg, lg_rest)[n]
                prios = prio[0:ROWS, :].unsqueeze(1).broadcast_to(many)
                if n == 0:
                    wait_read(dve, use(S, "logits"))
                    route_from(1)
                else:
                    route_from(7)
                done(dve.tensor_reduce(best[:, n, :], left[:, :, :], AX.X, ALU.max))
                done(dve.tensor_tensor(tie[:, :, :], left[:, :, :], wide(best[:, n, :], E_), ALU.is_equal))
                done(dve.tensor_tensor(tie[:, :, :], tie[:, :, :], prios, ALU.mult))
                done(dve.tensor_reduce(first_tie[:, :], tie[:, :, :], AX.X, ALU.max))
                done(dve.tensor_tensor(chosen[:, n, :, :], tie[:, :, :], wide(first_tie[:, :], E_),
                                       ALU.is_equal))
                if n == 0:
                    done(dve.scalar_tensor_tensor(out=lg_rest[:, :, :], in0=chosen[:, 0, :, :],
                                                  scalar=-BIG, in1=lg[:, :, :],
                                                  op0=ALU.mult, op1=ALU.add))

            def exponents(S):
                def done(instruction):
                    step_done(S, instruction)

                route_from(12)
                done(dve.tensor_tensor(expo[:, :, 0:E_], lg[:, :, :], wide(best[:, 0, :], E_), ALU.subtract))
                done(dve.tensor_tensor(expo[:, :, E_], best[:, 1, :], best[:, 0, :], ALU.subtract))
                assert routed_steps == EXPO_AT

            def second_gap(S):
                def done(instruction):
                    step_done(S, instruction)

                route_from(EXPO_AT)
                dve.wait_ge(expo_ready, S.count("T", 1))
                done(dve.tensor_reduce(expo_sum[:, :], expo[:, :, 0:E_], AX.X, ALU.add))
                done(dve.reciprocal(expo_inv[:, :], expo_sum[:, :]))
                done(dve.scalar_tensor_tensor(out=gap[:, :], in0=expo[:, :, E_], scalar=1.0,
                                              in1=expo_inv[:, :], op0=ALU.subtract, op1=ALU.mult))
                assert routed_steps == GAP_AT

            def weigh(S):
                def done(instruction):
                    step_done(S, instruction)

                route_from(GAP_AT)
                dve.wait_ge(gap_ready, S.count("T", 1))
                done(dve.tensor_scalar(gap[:, :], gap_exp[:, :], 1.0, None, ALU.add))
                done(dve.reciprocal(share[:, 0, :], gap[:, :]))
                done(dve.tensor_tensor(share[:, 1, :], gap_exp[:, :], share[:, 0, :], ALU.mult))
                done(dve.tensor_tensor(wsum[:, :, :, :], chosen[:, :, :, :],
                                       share[:, :, :].unsqueeze(3).broadcast_to([ROWS, 2, G, E_]), ALU.mult))
                done(dve.tensor_tensor(wts[:, :, :], wsum[:, 0, :, :], wsum[:, 1, :, :], ALU.add))
                assert routed_steps == WEIGHTS_AT

            def pair_weights(S):
                def done(instruction):
                    step_done(S, instruction)

                route_from(WEIGHTS_AT)
                done(dve.tensor_copy(wts_hi[:, :, :], wts[:, :, :]))
                both = [ROWS, G, 2, E_]
                pairs = wts_pair[:, :, :].rearrange("p g (k e) -> p g k e", k=2)
                high = wts_hi[:, :, :].bitcast(F32).unsqueeze(2).broadcast_to(both)
                done(dve.tensor_copy(pairs[:, :, :, 0:E_], high))
                done(dve.tensor_tensor(pairs[:, :, :, E_:2 * E_], wts[:, :, :].unsqueeze(2).broadcast_to(both),
                                       high, ALU.subtract))
                assert routed_steps == ROUTE

            def body(S):
                for j in range(NT):
                    if (S.at, j) == PREPARE_AT:
                        prepare()
                    if j == 1 and S.runs("X"):
                        k = S.ring("X")
                        dve.wait_ge(pixels_loaded[k], 2 * S.ring_dma("X"))
                        if S.has("X", 1):
                            dve.wait_ge(patches_ready, S.count("X", 1, back=1))
                        dve.tensor_copy(by_patch[:, :].rearrange("r (w p q) -> r p w q", p=PATCH, q=PATCH),
                                        pixels[:, k, :].rearrange("r (p w q) -> r p w q", p=PATCH, q=PATCH)
                                        ).then_inc(by_patch_ready, 1)
                    if j == 1 and S.runs("P"):
                        dve.wait_ge(h2_ready, S.count("P", 1))
                        sum_tokens(S, "P", 2, h2[:, S.ring("P"), :])
                    if j == 2 and S.runs("E"):
                        wait_read(dve, use(S, "tokens"))
                        sum_tokens(S, "E", 1, h1[:, S.ring("E"), :])
                    if S.runs("T"):
                        if j == 3:
                            choose(S, 0)
                        if j == 4:
                            exponents(S)
                        if j == 5:
                            second_gap(S)
                        if j == 6:
                            pair_weights(S)
                    if j < CHUNKS and S.runs("F"):
                        u = use(S, "spread", j)
                        dve.wait_ge(filled, u.filled())
                        wait_read(dve, use(S, "hidden2", j))
                        dve.tensor_tensor(scaled[:, j % 2, :], act2[:, j % 2, :], work[u.bank][:, 0:HALF],
                                          ALU.mult).then_inc(drained[u.bank], 1)
                    if j == 0 and S.runs("P"):
                        for i in range(2):
                            u = use(S, "attn", i)
                            gs = slice(i * (G // 2), (i + 1) * (G // 2))
                            src = work[u.bank][0:ROWS, 0:(G // 2) * (D + 1)].rearrange(
                                "p (g d) -> p g d", d=D + 1)
                            dve.wait_ge(filled, u.filled())
                            dve.reciprocal(inv_sum[:, gs], src[:, :, D]).then_inc(sums_inverted, 1)
                            dve.wait_ge(sums_inverted, S.count("P", 2, i + 1))
                            if S.has("P", 1):
                                dve.wait_ge(h2_ready, S.count("P", 1, back=1))
                            dve.tensor_tensor(groups(attn[:, :])[:, gs, :], src[:, :, 0:D],
                                              wide(inv_sum[:, :])[:, gs, :], ALU.mult
                                              ).then_inc(drained[u.bank], 1)
                    if S.runs("A"):
                        for t in score_tiles(j):
                            n = width(t)
                            for h in range(2):
                                u = use(S, "scores", t, h)
                                dve.wait_ge(filled, u.filled())
                                dve.tensor_reduce(row_max[0:n, t, h:h + 1], work[u.bank][0:n, 0:HALF],
                                                  AX.X, ALU.max).then_inc(drained[u.bank], 1)
                            for h in range(2):
                                wait_read(dve, use(S, "scores", t, h))
                            if S.has("A", 1):
                                dve.wait_ge(diag_ready, S.count("A", NT, t + 1, back=1))
                            dve.tensor_reduce(minus_max[0:n, t:t + 1], row_max[0:n, t, :], AX.X, ALU.max,
                                              negate=True).then_inc(max_ready, 1)
                    if j == 1 and S.runs("T"):
                        for h in range(2):
                            u = use(S, "router", h)
                            cols = slice(h * HALF, (h + 1) * HALF)
                            dve.wait_ge(routed_hi, S.count("T", 2, h + 1))
                            dve.scalar_tensor_tensor(out=routed[RH:2 * RH, cols],
                                                     in0=work[u.bank][RH:2 * RH, 0:HALF], scalar=0.0,
                                                     in1=routed[RH:2 * RH, cols].bitcast(F32),
                                                     op0=ALU.max, op1=ALU.subtract
                                                     ).then_inc(drained[u.bank], 1)
                    if j == 2 and S.runs("P"):
                        variance(S, "P", 2)
                    if j == 2 and S.runs("T"):
                        read_logits(S)
                    if j == 3 and S.runs("A"):
                        u = use(S, "values")
                        k = S.ring("A")
                        full = NT - 1
                        n = width(full)
                        dve.wait_ge(filled, u.filled())
                        dve.tensor_copy(values[:, k, 0:full, 0:D],
                                        work[u.bank][:, 0:full * D].rearrange("p (t d) -> p t d", d=D))
                        dve.tensor_copy(values[0:n, k, full, 0:D], work[u.bank][0:n, full * D:NT * D]
                                        ).then_inc(drained[u.bank], 1)
                    if j == 3 and S.runs("T"):
                        choose(S, 1)
                    if j == 3 and S.runs("E"):
                        variance(S, "E", 1)
                    if j == 5:
                        if S.runs("E"):
                            low_half(S, "E", "norm1", pair1, hi1_ready)
                        if S.runs("P"):
                            low_half(S, "P", "norm2", pair2, hi2_ready)
                    if j == 5 and S.runs("T"):
                        weigh(S)
                    if j == 6:
                        if S.runs("A"):
                            for h in range(2):
                                u = use(S, "shifted", h)
                                cols = slice(h * HALF, (h + 1) * HALF)
                                k = S.ring("A")
                                dve.wait_ge(shifted_hi, S.count("A", 2, h + 1))
                                dve.tensor_tensor(shifted[1][:, k, cols], work[u.bank][:, 0:HALF],
                                                  shifted[0][:, k, cols].bitcast(F32), ALU.subtract
                                                  ).then_inc(drained[u.bank], 1)
                        if S.runs("F"):
                            u = use(S, "back")
                            k = S.ring("F")
                            dve.wait_ge(filled, u.filled())
                            if S.has("F", RING):
                                dve.wait_ge(stored[k], S.ring_dma("F", back=RING))
                            dve.tensor_tensor(result[:, k, :], work[u.bank][0:ROWS, :], h2[:, k, :], ALU.add
                                              ).then_inc(drained[u.bank], 1)

            run_steps(dve, body)

    return nc


_INS = ["x", "txt", "L0_tok_W", "L0_tok_b", "L0_attn_Wq", "L0_attn_bq", "L0_attn_Wk", "L0_attn_bk",
        "L0_attn_Wv", "L0_attn_bv", "L0_ffn_router_w1", "L0_ffn_router_b1", "L0_ffn_router_w2",
        "L0_ffn_router_b2", "L0_ffn_expert_w1", "L0_ffn_expert_b1", "L0_ffn_expert_w2",
        "L0_ffn_expert_b2", "L0_ffn_expert_w3", "L0_ffn_expert_b3"]


def kernel(**inputs):
    import numpy as np
    import concourse.bacc as bacc
    from concourse.bass_utils import run_bass_kernel_spmd

    nc = bacc.Bacc("TRN2", target_bir_lowering=False, num_devices=1)
    arrays, args = {}, []
    for name in _INS:
        a = np.ascontiguousarray(inputs[name])
        arrays[f"in_{name}"] = a
        args.append(nc.dram_tensor(f"in_{name}", a.shape, mybir.dt.from_np(a.dtype), kind="ExternalInput").ap())
    out = nc.dram_tensor("out", (BATCH, TOK, D), F32, kind="ExternalOutput").ap()
    encoder_kernel(nc, *args, out)
    r = run_bass_kernel_spmd(nc, [arrays], core_ids=[0])
    return r.results[0]["out"]
```

```python
from contextlib import ExitStack

import concourse.bass as bass
from concourse import mybir

F32 = mybir.dt.float32
F32R = mybir.dt.float32r
ALU = mybir.AluOpType
ACT = mybir.ActivationFunctionType
AX = mybir.AxisListType

P = 128
BATCH = 32
D = 64
IMG = 224
PATCH = 8
SIDE = IMG // PATCH
WP2 = SIDE // 4
HROW = IMG // 2
TXT = 32
NIMG = SIDE * SIDE // 2
TOK = SIDE * SIDE + TXT
HALF = TOK // 2
ROWS = 102
TT = HALF // ROWS
G = 2 * TT
NT = -(-TOK // P)
E_ = 6
RH = 32
PAIRS = E_ // 2
CHUNKS = 2 * PAIRS
EPS = 1e-5
SCALE = D ** -0.5
BIG = 3.0e38
RING = 3
LAG = dict(X=0, E=1, A=2, B=3, P=4, T=5, F=6)
DEPTH = max(LAG.values())
WORK = 5


def width(t):
    return min(P, TOK - P * t)


def score_tiles(j):
    return ((0,), (1,), (2,), (3,), (4, 5), (6,), ())[j]


def max_tiles(j):
    return {3: (range(0, 4),), 5: (range(4, 6), range(6, 7))}.get(j, ())


MAX_GROUPS = 3


def bank_users(j):
    out = []
    if j == 0:
        out += [("P", "mixed", 0), ("P", "mixed", 1), ("F", "hidden1", 0)]
    out += [("B", "scores_t", j, 0), ("B", "scores_t", j, 1)]
    out += [("A", "scores", t, h) for t in score_tiles(j) for h in (0, 1)]
    if j < CHUNKS:
        out += [("F", "spread", j), ("F", "hidden2", j)]
    if j + 1 < CHUNKS:
        out += [("F", "hidden1", j + 1)]
    if j == 0:
        out += [("E", "embed"), ("P", "attn", 0), ("P", "attn", 1)]
    out += {
        0: [("T", "router", 0), ("T", "router", 1)],
        1: [("E", "tokens"), ("T", "logits")],
        2: [("X", "patches")],
        3: [],
        4: [("A", "keys", 0), ("A", "keys", 1)],
        5: [("P", "norm2", 0), ("P", "norm2", 1), ("E", "norm1", 0), ("E", "norm1", 1)],
        6: [("E", "query", 0), ("E", "query", 1), ("A", "shifted", 0), ("A", "shifted", 1),
            ("T", "weights", 0), ("T", "weights", 1), ("F", "back")],
    }[j]
    return out


class Use:

    def __init__(self, bank, filled, drained, step):
        self.bank, self.filled_at, self.drained_at, self.step = bank, filled, drained, step

    def filled(self):
        return self.filled_at + self.step.turn * self.step.filled_per_turn

    def drained(self):
        return self.drained_at + self.step.turn * self.step.drained_per_turn[self.bank]

    def read(self):
        return self.drained() + 1


class Step:

    def __init__(self, at, turn=0):
        self.at, self.turn = at, turn

    def runs(self, stage):
        return 0 <= self.at - LAG[stage] < BATCH

    def ring(self, stage):
        return (self.at - LAG[stage]) % RING

    def image(self, stage):
        return self.at - LAG[stage] + RING * self.turn

    def has(self, stage, back):
        return self.at - LAG[stage] - back >= 0

    def count(self, stage, each, part=None, back=0):
        b = self.at - LAG[stage] - back
        return b * each + (each if part is None else part) + self.turn * (RING * each)

    def ring_dma(self, stage, back=0):
        return 16 * ((self.at - LAG[stage] - back) // RING + 1) + self.turn * 16


FIRST_LOOPED = DEPTH + 1
TURNS = (BATCH - FIRST_LOOPED) // RING
AFTER_LOOP = FIRST_LOOPED + TURNS * RING
LAST = BATCH + DEPTH


def plan():
    uses, filled, drained, turn = {}, 0, [0] * WORK, 0
    in_step = [name for j in range(NT) for name in bank_users(j)]

    def walk(steps):
        nonlocal filled, turn
        for s in steps:
            in_place = FIRST_LOOPED - 1 <= s < AFTER_LOOP
            at = (s - FIRST_LOOPED) % RING * len(in_step)
            for n, (stage, *name) in enumerate(in_step):
                if Step(s).runs(stage):
                    turn = (at + n if in_place else turn + 1) % WORK
                    bank = turn
                    uses[s, tuple(name)] = (bank, filled + 1, drained[bank])
                    filled += 1
                    drained[bank] += 1

    walk(range(FIRST_LOOPED))
    before, were = filled, list(drained)
    walk(range(FIRST_LOOPED, FIRST_LOOPED + RING))
    per_turn = filled - before
    drained_per_turn = [a - b for a, b in zip(drained, were)]
    filled += (TURNS - 1) * per_turn
    for k in range(WORK):
        drained[k] += (TURNS - 1) * drained_per_turn[k]
    walk(range(AFTER_LOOP, LAST))
    return uses, per_turn, drained_per_turn


USES, FILLED_PER_TURN, DRAINED_PER_TURN = plan()
Step.filled_per_turn = FILLED_PER_TURN
Step.drained_per_turn = DRAINED_PER_TURN


def use(step, *name):
    return Use(*USES[step.at, name], step)


def last_use(step, *name):
    if step.at != AFTER_LOOP and step.at != FIRST_LOOPED:
        return Use(*USES[step.at - 1, name], step)
    turns = 1 if step.at == FIRST_LOOPED else 1 - TURNS
    at = FIRST_LOOPED + RING - 1
    bank, filled, drained = USES[at, name]
    return Use(bank, filled - turns * FILLED_PER_TURN, drained - turns * DRAINED_PER_TURN[bank], step)


for _name in (("query", 1), ("shifted", 1), ("weights", 1), ("norm2", 1), ("keys", 1)):
    _u = last_use(Step(FIRST_LOOPED), *_name)
    assert (_u.bank, _u.filled_at, _u.drained_at) == USES[FIRST_LOOPED - 1, _name]


def run_steps(eng, body):
    for s in range(FIRST_LOOPED):
        body(Step(s))
    with eng.Fori(0, TURNS) as turn:
        for u in range(RING):
            body(Step(FIRST_LOOPED + u, turn))
    for s in range(AFTER_LOOP, LAST):
        body(Step(s))


def encoder_kernel(nc, x, txt, tok_W, tok_b, Wq, bq, Wk, bk, Wv, bv, r_w1, r_b1, r_w2, r_b2,
                   e_w1, e_b1, e_w2, e_b2, e_w3, e_b3, out):
    ctx = ExitStack()
    with ctx:
        def sb(name, shape, dt=F32):
            return ctx.enter_context(nc.sbuf_tensor(name, shape, dt))

        def sem(name):
            return ctx.enter_context(nc.semaphore(name))

        work = [ctx.enter_context(nc.psum_tensor(f"work{k}", [P, 512], F32)) for k in range(WORK)]
        ps_attn = ctx.enter_context(nc.psum_tensor("ps_attn", [P, 2, 512], F32))
        ps_moe = ctx.enter_context(nc.psum_tensor("ps_moe", [P, 512], F32))

        ident = sb("ident", [P, P])
        ones_r = sb("ones_r", [P, P], F32R)
        center = sb("center", [D + 1, 2 * D])
        prio = sb("prio", [P, E_])
        minus_half = sb("minus_half", [P, G])
        one_of_d = sb("one_of_d", [P, G])
        raw_tok = sb("raw_tok", [D, 2 * D])
        tok_bias = sb("tok_bias", [P, 1])
        value_w = sb("value_w", [P, D + 1])
        embed_w = sb("embed_w", [P, P])
        NF = 2 * D + 2 * RH + E_ * D
        QC, VC, RC, EC = 0, D, 2 * D, 2 * D + 2 * RH
        raw_first = sb("raw_first", [D + 1, NF])
        raw_k = sb("raw_k", [D + 1, D])
        query_t = sb("query_t", [D, 2 * D])
        key_t = sb("key_t", [D, 2 * D])
        score_w = [sb("score_w_hi", [P, P], F32R), sb("score_w_lo", [P, P], F32R)]
        first_w = [sb("first_w_hi", [P, NF], F32R), sb("first_w_lo", [P, NF], F32R)]
        w2 = sb("w2", [P, PAIRS, P])
        b2 = sb("b2", [P, PAIRS])
        w3 = sb("w3", [P, PAIRS, D])
        raw_r2 = sb("raw_r2", [2 * RH, E_])
        router2 = sb("router2", [2 * RH, 2 * E_], F32R)
        router_bias = sb("router_bias", [ROWS, E_])
        raw_b3 = sb("raw_b3", [4 * E_, D])
        b3_hi = sb("b3_hi", [4 * E_, D], F32R)
        b3_lo = sb("b3_lo", [4 * E_, D])
        b3_low_rows = sb("b3_low_rows", [4 * E_, D])
        is_hi_row = sb("is_hi_row", [4 * E_, D])
        is_lo_row = sb("is_lo_row", [4 * E_, D])
        b3 = sb("b3", [4 * E_, D], F32R)
        raw_pick = sb("raw_pick", [4 * E_, PAIRS, 2, D])
        pick = sb("pick", [4 * E_, PAIRS * P], F32R)

        pixels = sb("pixels", [2 * SIDE, RING, PATCH * HROW])
        by_patch = sb("by_patch", [2 * SIDE, PATCH * HROW])
        text = sb("text", [TXT // 2, RING, 2 * D])
        patches = sb("patches", [P, NIMG])
        embed_t = sb("embed_t", [P, HALF])
        h1 = sb("h1", [ROWS, RING, G * D])
        stat = {k: [sb(f"{n}{k}", [ROWS, G]) for n in ("total", "mean", "squares", "var", "rstd")]
                for k in (1, 2)}
        xc = {k: sb(f"xc{k}", [ROWS, G * D]) for k in (1, 2)}
        sq = {k: sb(f"sq{k}", [ROWS, G * D]) for k in (1, 2)}
        xn = {k: sb(f"xn{k}", [ROWS, G * D]) for k in (1, 2)}
        pair1 = sb("pair1", [P, RING, TOK], F32R)
        pair2 = sb("pair2", [P, RING, TOK], F32R)
        query_hi = sb("query_hi", [P, RING, TOK], F32R)
        keys = sb("keys", [P, RING, NT, 2 * D], F32R)
        row_max = sb("row_max", [P, NT, 2])
        minus_max = sb("minus_max", [P, NT])
        max_diag = sb("max_diag", [P, TOK], F32R)
        shifted = [sb("shifted_hi", [P, RING, TOK], F32R), sb("shifted_lo", [P, RING, TOK], F32R)]
        probs = sb("probs", [P, 2, TOK])
        probs_hi = sb("probs_hi", [P, 3, TOK], F32R)
        probs_lo = sb("probs_lo", [P, 3, TOK], F32R)
        blend_t = sb("blend_t", [P, TOK])
        attn_t = sb("attn_t", [D + 1, TOK])
        inv_sum = sb("inv_sum", [ROWS, G])
        attn = sb("attn", [ROWS, G * D])
        h2 = sb("h2", [ROWS, RING, G * D])
        routed = sb("routed", [2 * RH, TOK], F32R)
        lg = sb("lg", [ROWS, G, E_])
        lg_hi = sb("lg_hi", [ROWS, G, E_])
        lg_rest = sb("lg_rest", [ROWS, G, E_])
        best = sb("best", [ROWS, 2, G])
        tie = sb("tie", [ROWS, G, E_])
        first_tie = sb("first_tie", [ROWS, G])
        chosen = sb("chosen", [ROWS, 2, G, E_])
        expo = sb("expo", [ROWS, G, E_ + 1])
        expo_sum = sb("expo_sum", [ROWS, G])
        expo_inv = sb("expo_inv", [ROWS, G])
        gap = sb("gap", [ROWS, G])
        gap_exp = sb("gap_exp", [ROWS, G])
        share = sb("share", [ROWS, 2, G])
        wsum = sb("wsum", [ROWS, 2, G, E_])
        wts = sb("wts", [ROWS, G, E_])
        wts_hi = sb("wts_hi", [ROWS, G, E_], F32R)
        wts_pair = sb("wts_pair", [ROWS, G, 4 * E_])
        weights_t = sb("weights_t", [4 * E_, RING, TOK], F32R)
        act1 = sb("act1", [P, 2, HALF])
        act2 = sb("act2", [P, 2, HALF])
        scaled = sb("scaled", [P, 2, HALF])
        moe_t = sb("moe_t", [D, TOK])
        result = sb("result", [ROWS, RING, G * D])

        tok_loaded = sem("tok_loaded")
        weights_loaded = sem("weights_loaded")
        consts_made = sem("consts_made")
        prep_filled = sem("prep_filled")
        prep_copied = sem("prep_copied")
        pixels_loaded = [sem(f"pixels_loaded{k}") for k in range(RING)]
        text_loaded = [sem(f"text_loaded{k}") for k in range(RING)]
        stored = [sem(f"stored{k}") for k in range(RING)]
        filled = sem("filled")
        drained = [sem(f"drained{k}") for k in range(WORK)]
        by_patch_ready = sem("by_patch_ready")
        patches_ready = sem("patches_ready")
        total_ready = {k: sem(f"total_ready{k}") for k in (1, 2)}
        norm_step = {k: sem(f"norm_step{k}") for k in (1, 2)}
        var_step = {k: sem(f"var_step{k}") for k in (1, 2)}
        hi1_ready = sem("hi1_ready")
        hi2_ready = sem("hi2_ready")
        max_ready = sem("max_ready")
        diag_ready = sem("diag_ready")
        shifted_hi = sem("shifted_hi")
        attended = sem("attended")
        blend_copied = sem("blend_copied")
        lo_ready = [sem("lo_ready0"), sem("lo_ready1")]
        sums_inverted = sem("sums_inverted")
        h2_ready = sem("h2_ready")
        routed_hi = sem("routed_hi")
        route_step = sem("route_step")
        expo_ready = sem("expo_ready")
        gap_ready = sem("gap_ready")
        chunk_done = sem("chunk_done")
        moe_copied = sem("moe_copied")
        EXPO_AT, GAP_AT, ROUTE = 14, 17, 25
        PREPARE_AT = (1, 6)
        N_LOADS = 29
        N_CONSTS = 16 + E_
        N_PREP = 21

        block = ctx.enter_context(nc.Block())

        key_banks = (range(0, 4), range(4, NT))

        def groups(ap):
            return ap.rearrange("p (g d) -> p g d", d=D)

        def wide(stat_ap, n=D):
            return stat_ap.unsqueeze(2).broadcast_to([ROWS, G, n])

        def wait_read(eng, u):
            eng.wait_ge(drained[u.bank], u.read())

        def low_probs(eng, S, t, h):
            n, cols = width(t), slice(h * HALF, (h + 1) * HALF)
            wait_read(eng, use(S, "scores_t", t, h))
            eng.tensor_tensor(probs_lo[0:n, t % 3, cols], probs[0:n, t % 2, cols],
                              probs_hi[0:n, t % 3, cols].bitcast(F32), ALU.subtract
                              ).then_inc(lo_ready[h], 1)

        @block.sync
        def _(sp):
            def load(dst, src):
                sp.dma_start(dst, src).then_inc(weights_loaded, 16)

            def load_image(S):
                if S.has("X", RING):
                    sp.wait_ge(by_patch_ready, S.count("X", 1, back=RING))
                    sp.wait_ge(patches_ready, S.count("X", 1, back=RING))
                b = S.image("X")
                k = S.ring("X")
                rows = x[b, 0].rearrange("(r p) w -> r p w", p=PATCH)
                for h in range(2):
                    sp.dma_start(pixels[h * SIDE:(h + 1) * SIDE, k, :].rearrange("r (p w) -> r p w", p=PATCH),
                                 rows[:, :, h * HROW:(h + 1) * HROW]).then_inc(pixels_loaded[k], 16)
                sp.dma_start(text[:, k, :], txt[b].rearrange("(r p) d -> r (p d)", p=2)
                             ).then_inc(text_loaded[k], 16)

            load_image(Step(0))
            for k in range(2):
                sp.dma_start(raw_tok[:, k * D:(k + 1) * D], tok_W).then_inc(tok_loaded, 16)
                sp.dma_start(tok_bias[k * D:(k + 1) * D, :], tok_b.rearrange("(d o) -> d o", o=1)
                             ).then_inc(tok_loaded, 16)
            load_image(Step(1))
            for c, (w, b) in ((QC, (Wq, bq)), (VC, (Wv, bv)), (RC, (r_w1, r_b1)), (RC + RH, (r_w1, r_b1))):
                n = w.shape[1]
                load(raw_first[0:D, c:c + n], w)
                load(raw_first[D:D + 1, c:c + n], b.rearrange("(o d) -> o d", o=1))
            load(raw_first[0:D, EC:NF].rearrange("p (e h) -> p e h", e=E_), e_w1.rearrange("e d h -> d e h"))
            load(raw_first[D:D + 1, EC:NF], e_b1.rearrange("(o e) h -> o (e h)", o=1))
            load(raw_k[0:D, :], Wk)
            load(raw_k[D:D + 1, :], bk.rearrange("(o d) -> o d", o=1))
            sp.wait_ge(consts_made, 2)
            for k in range(2):
                load(w2[k * D:(k + 1) * D, :, k * D:(k + 1) * D],
                     e_w2.rearrange("(q k) h f -> k h q f", k=2)[k])
                for q in range(PAIRS):
                    load(b2[k * D:(k + 1) * D, q:q + 1], e_b2[2 * q + k].rearrange("(f o) -> f o", o=1))
                load(w3[k * D:(k + 1) * D, :, :], e_w3.rearrange("(q k) f o -> k f q o", k=2)[k])
                load(raw_r2[k * RH:(k + 1) * RH, :], r_w2)
            load(router_bias[:, :], r_b2.rearrange("(o e) -> o e", o=1).broadcast_to([ROWS, E_]))
            for k in range(4):
                load(raw_b3[k * E_:(k + 1) * E_, :], e_b3)

            def body(S):
                if S.runs("X") and S.at > 1:
                    load_image(S)
                if S.runs("F"):
                    b = S.image("F")
                    k = S.ring("F")
                    wait_read(sp, use(S, "back"))
                    sp.dma_start(out[b].rearrange("(t r p) d -> r t (p d)", t=TT, r=ROWS),
                                 result[:, k, :].rearrange("r (t q) -> r t q", t=TT)
                                 ).then_inc(stored[k], 16)

            run_steps(sp, body)
            for k in range(RING):
                sp.wait_ge(stored[k], 16 * len(range(k, BATCH, RING)))

        @block.gpsimd
        def _(pool):
            pool.memset(center[D:D + 1, :], 1.0).then_inc(consts_made, 1)
            pool.wait_ge(consts_made, 1)
            pool.memset(w2[:, :, :], 0.0).then_inc(consts_made, 1)
            pool.memset(embed_w[:, :], 0.0).then_inc(consts_made, 1)
            pool.memset(ident[:, :], 0.0).then_inc(consts_made, 1)
            pool.memset(center[0:D, :], -1.0 / D).then_inc(consts_made, 1)
            pool.memset(raw_pick[:, :, :, :], 0.0).then_inc(consts_made, 1)
            pool.memset(is_hi_row[:, :], 1.0).then_inc(consts_made, 1)
            pool.memset(minus_half[:, :], -0.5).then_inc(consts_made, 1)
            pool.memset(one_of_d[:, :], 1.0 / D).then_inc(consts_made, 1)
            for e in range(E_):
                pool.memset(prio[:, e:e + 1], float(E_ - e)).then_inc(consts_made, 1)
            pool.memset(value_w[:, :], 1.0).then_inc(consts_made, 1)
            pool.memset(max_diag[:, :].bitcast(F32), 0.0).then_inc(consts_made, 1)
            made = 11 + E_
            pool.wait_ge(consts_made, made)
            pool.affine_select(out=ident[:, :], in_=ident[:, :], compare_op=ALU.not_equal, fill=1.0,
                               base=0, pattern=[[-1, P]], channel_multiplier=1).then_inc(consts_made, 1)
            pool.affine_select(out=center[0:D, :].rearrange("p (k d) -> p k d", k=2),
                               in_=center[0:D, :].rearrange("p (k d) -> p k d", k=2),
                               compare_op=ALU.not_equal, fill=1.0 - 1.0 / D, base=0,
                               pattern=[[0, 2], [-1, D]], channel_multiplier=1).then_inc(consts_made, 1)
            pool.affine_select(out=is_hi_row[:, :], in_=is_hi_row[:, :], compare_op=ALU.is_ge, fill=0.0,
                               base=2 * E_ - 1, pattern=[[0, D]], channel_multiplier=-1
                               ).then_inc(consts_made, 1)
            for k in range(2):
                pool.affine_select(out=raw_pick[:, :, :, :], in_=raw_pick[:, :, :, :],
                                   compare_op=ALU.not_equal, fill=1.0, base=-E_ * k,
                                   pattern=[[-2, PAIRS], [-1, 2], [0, D]], channel_multiplier=1
                                   ).then_inc(consts_made, 1)
                pool.wait_ge(consts_made, made + 4 + k)

            def norm(S, stage, k, x_ap):
                step = norm_step[k]
                total, mean = stat[k][:2]
                pool.wait_ge(total_ready[k], S.count(stage, 1))
                if S.has(stage, 1):
                    pool.wait_ge(var_step[k], S.count(stage, 2, 1, back=1))
                pool.tensor_tensor(mean[:, :], total[:, :], one_of_d[0:ROWS, :], ALU.mult).then_inc(step, 1)
                pool.wait_ge(step, S.count(stage, 5, 1))
                pool.tensor_tensor(groups(xc[k][:, :]), groups(x_ap), wide(mean[:, :]), ALU.subtract
                                   ).then_inc(step, 1)
                pool.wait_ge(step, S.count(stage, 5, 2))
                pool.tensor_tensor(sq[k][:, :], xc[k][:, :], xc[k][:, :], ALU.mult).then_inc(step, 1)

            def norm_end(S, stage, k):
                step = norm_step[k]
                _, _, _, var, rstd = stat[k]
                pool.wait_ge(var_step[k], S.count(stage, 2))
                pool.tensor_tensor(rstd[:, :], var[:, :], minus_half[0:ROWS, :], ALU.pow).then_inc(step, 1)
                pool.wait_ge(step, S.count(stage, 5, 4))
                if S.has(stage, 1):
                    pool.wait_ge({1: hi1_ready, 2: hi2_ready}[k], S.count(stage, 2, back=1))
                pool.tensor_tensor(groups(xn[k][:, :]), groups(xc[k][:, :]), wide(rstd[:, :]), ALU.mult
                                   ).then_inc(step, 1)

            def body(S):
                maxima_made = 0
                for j in range(NT):
                    if S.runs("B"):
                        low_probs(pool, S, j, 1)
                    if j == 1 and S.runs("P"):
                        norm(S, "P", 2, h2[:, S.ring("P"), :])
                    if j == 2 and S.runs("E"):
                        norm(S, "E", 1, h1[:, S.ring("E"), :])
                    if j == 3 and S.runs("P"):
                        norm_end(S, "P", 2)
                    if j == 4 and S.runs("E"):
                        norm_end(S, "E", 1)
                    if S.runs("A"):
                        for tiles in max_tiles(j):
                            t, m, n = tiles[0], len(tiles), width(tiles[0])
                            maxima_made += 1
                            pool.wait_ge(max_ready, S.count("A", MAX_GROUPS, maxima_made))
                            if t == 0 and S.has("A", 1):
                                pool.wait_ge(shifted_hi, S.count("A", 2, back=1))
                            pool.tensor_tensor(
                                max_diag[0:n, t * P:t * P + m * n].rearrange("p (t q) -> p t q", t=m),
                                ident[0:n, 0:n].unsqueeze(1).broadcast_to([n, m, n]),
                                minus_max[0:n, t:t + m].unsqueeze(2).broadcast_to([n, m, n]), ALU.mult
                                ).then_inc(diag_ready, 1)

            run_steps(pool, body)

        @block.tensor
        def _(pe):
            pe.wait_ge(consts_made, N_CONSTS)
            pe.wait_ge(tok_loaded, 16 * 4)
            pe.matmul(ps_moe[:, 0:D], raw_tok[:, :], ident[0:D, 0:D], start=True, stop=True
                      ).then_inc(prep_filled, 1)

            def prepare():
                pe.wait_ge(weights_loaded, 16 * N_LOADS)
                pe.matmul(ps_moe[0:D, P:2 * P], raw_first[:, QC:QC + D], center[:, :], start=True, stop=True)
                pe.matmul(ps_moe[0:D, 2 * P:3 * P], raw_k[:, :], center[:, :], start=True, stop=True)
                pe.matmul(ps_attn[:, 0, 0:EC], center[:, :], raw_first[:, 0:EC], start=True, stop=True)
                pe.matmul(ps_attn[:, 1, 0:NF - EC], center[:, :], raw_first[:, EC:NF], start=True, stop=True
                          ).then_inc(prep_filled, 1)
                pe.wait_ge(prep_copied, 4)
                pe.matmul(ps_moe[:, 3 * P:4 * P], query_t[:, :], key_t[:, :], start=True, stop=True
                          ).then_inc(prep_filled, 1)
                pe.wait_ge(prep_copied, 6)

            def take(S, *name, after=()):
                u = use(S, *name)
                least = {u.bank: (u.drained_at, u.drained)} if u.drained_at > 0 else {}
                for v in after:
                    if v.drained_at + 1 > least.get(v.bank, (0,))[0]:
                        least[v.bank] = (v.drained_at + 1, v.read)
                for bank, (_, count) in least.items():
                    pe.wait_ge(drained[bank], count())
                return work[u.bank]

            def two_passes(dst, w, c, n, rhs):
                pe.matmul(dst, w[0][:, c:c + n], rhs, start=True, stop=False)
                return pe.matmul(dst, w[1][:, c:c + n], rhs, start=False, stop=True)

            def attend(S, t):
                n = width(t)
                for h in range(2):
                    pe.wait_ge(lo_ready[h], S.count("B", NT, t + 1))
                    if t == 0 and S.has("B", 1):
                        pe.wait_ge(blend_copied, S.count("B", 2, h + 1, back=1))
                    for part, p in enumerate((probs_hi, probs_lo)):
                        mm = pe.matmul(ps_attn[:, h, 0:HALF], keys[0:n, S.ring("B"), t, :],
                                       p[0:n, t % 3, h * HALF:(h + 1) * HALF],
                                       start=(t == 0 and part == 0), stop=(t == NT - 1 and part == 1))
                    mm.then_inc(attended, 1)

            def hidden1(S, c):
                h, q = divmod(c, PAIRS)
                bank = take(S, "hidden1", c)
                two_passes(bank[:, 0:HALF], first_w, EC + q * P, P,
                           pair2[:, S.ring("F"), h * HALF:(h + 1) * HALF]).then_inc(filled, 1)

            def experts_out(S, c):
                h, q = divmod(c, PAIRS)
                wait_read(pe, use(S, "spread", c))
                if q == 0 and (h == 1 or S.has("F", 1)):
                    pe.wait_ge(moe_copied, S.count("F", 2, h, back=0))
                pe.matmul(ps_moe[0:D, 0:HALF], w3[:, q, :], scaled[:, c % 2, :], start=(q == 0), stop=False)
                if q == PAIRS - 1:
                    pe.matmul(ps_moe[0:D, 0:HALF], b3[:, :],
                              weights_t[:, S.ring("F"), h * HALF:(h + 1) * HALF],
                              start=False, stop=True).then_inc(chunk_done, 1)

            def body(S):
                for j in range(NT):
                    if (S.at, j) == PREPARE_AT:
                        prepare()
                    if (S.at, j) == (PREPARE_AT[0] + 1, 0):
                        pe.wait_ge(prep_copied, N_PREP)
                    h, q = divmod(j, PAIRS)
                    cols = slice(h * HALF, (h + 1) * HALF)
                    if j == 0 and S.runs("P"):
                        for half in range(2):
                            pe.wait_ge(blend_copied, S.count("P", 2, half + 1))
                            bank = take(S, "mixed", half)
                            pe.matmul(bank[0:D + 1, 0:HALF], value_w[:, :],
                                      blend_t[:, half * HALF:(half + 1) * HALF], start=True, stop=True
                                      ).then_inc(filled, 1)
                    if j == 0 and S.runs("F"):
                        hidden1(S, 0)
                    if S.runs("B"):
                        n, k = width(j), S.ring("B")
                        for half in range(2):
                            bank = take(S, "scores_t", j, half,
                                        after=[last_use(S, "shifted", half), last_use(S, "keys", half)]
                                        if j == 0 else [])
                            for part in range(2):
                                mm = pe.matmul(bank[0:n, 0:HALF], pair1[:, k, j * P:j * P + n],
                                               shifted[part][:, k, half * HALF:(half + 1) * HALF],
                                               start=(part == 0), stop=(part == 1))
                            mm.then_inc(filled, 1)
                    if S.runs("A"):
                        k = S.ring("A")
                        for t in score_tiles(j):
                            n = width(t)
                            for h in range(2):
                                bank = take(S, "scores", t, h,
                                            after=[last_use(S, "query", 0), last_use(S, "query", 1)]
                                            if (t, h) == (0, 0) else [])
                                pe.matmul(bank[0:n, 0:HALF], query_hi[:, k, t * P:t * P + n],
                                          pair1[:, k, h * HALF:(h + 1) * HALF],
                                          start=True, stop=True).then_inc(filled, 1)
                    if j >= 1 and S.runs("F") and S.runs("B"):
                        experts_out(S, j - 1)
                    if j < CHUNKS and S.runs("F"):
                        bank = take(S, "spread", j, after=[last_use(S, "weights", h)])
                        pe.matmul(bank[:, 0:HALF], pick[:, q * P:(q + 1) * P],
                                  weights_t[:, S.ring("F"), cols], start=True, stop=True
                                  ).then_inc(filled, 1)
                        bank = take(S, "hidden2", j, after=[use(S, "hidden1", j)])
                        pe.matmul(bank[:, 0:HALF], w2[:, q, :], act1[:, j % 2, :], start=True, stop=True
                                  ).then_inc(filled, 1)
                    if j + 1 < CHUNKS and S.runs("F"):
                        hidden1(S, j + 1)
                    if j >= 1 and S.runs("F") and not S.runs("B"):
                        experts_out(S, j - 1)
                    if j >= 1 and S.runs("B"):
                        attend(S, j - 1)
                    if j == 0 and S.runs("E"):
                        pe.wait_ge(patches_ready, S.count("E", 1))
                        bank = take(S, "embed")
                        pe.matmul(bank[:, 0:NIMG], embed_w[:, :], patches[:, :], start=True, stop=True
                                  ).then_inc(filled, 1)
                    if j == 0 and S.runs("P"):
                        for i in range(2):
                            bank = take(S, "attn", i, after=[use(S, "mixed", i)])
                            for g in range(G // 2):
                                c = (i * (G // 2) + g) * ROWS
                                mm = pe.transpose(bank[0:ROWS, g * (D + 1):(g + 1) * (D + 1)],
                                                  attn_t[:, c:c + ROWS], ident[0:D + 1, 0:D + 1])
                            mm.then_inc(filled, 1)
                    if j == 0 and S.runs("T"):
                        k = S.ring("T")
                        for h in range(2):
                            bank = take(S, "router", h, after=[last_use(S, "norm2", h)])
                            two_passes(bank[0:2 * RH, 0:HALF], first_w, RC, 2 * RH,
                                       pair2[:, k, h * HALF:(h + 1) * HALF]).then_inc(filled, 1)
                    if j == 1 and S.runs("E"):
                        bank = take(S, "tokens", after=[use(S, "embed")])
                        for t in range(TT):
                            mm = pe.transpose(bank[0:ROWS, t * P:(t + 1) * P],
                                              embed_t[:, t * ROWS:(t + 1) * ROWS], ident[:, :])
                        mm.then_inc(filled, 1)
                    if j == 1 and S.runs("T"):
                        bank = take(S, "logits", after=[use(S, "router", 0), use(S, "router", 1)])
                        for g in range(G):
                            mm = pe.matmul(bank[0:ROWS, g * 2 * E_:(g + 1) * 2 * E_],
                                           routed[:, g * ROWS:(g + 1) * ROWS], router2[:, :],
                                           start=True, stop=True)
                        mm.then_inc(filled, 1)
                    if j == 2 and S.runs("X"):
                        k = S.ring("X")
                        pe.wait_ge(by_patch_ready, S.count("X", 1))
                        pe.wait_ge(text_loaded[k], S.ring_dma("X"))
                        bank = take(S, "patches")
                        n = 2 * SIDE
                        pe.matmul(bank[:, 0:n], by_patch[:, 0:P], ident[0:n, 0:n], start=True, stop=True)
                        for w in range(1, WP2):
                            pe.transpose(bank[:, w * n:(w + 1) * n], by_patch[:, w * P:(w + 1) * P],
                                         ident[0:n, 0:n])
                        pe.transpose(bank[:, NIMG:HALF], text[:, k, :], ident[0:TXT // 2, 0:TXT // 2]
                                     ).then_inc(filled, 1)
                    if j == 4 and S.runs("A"):
                        k = S.ring("A")
                        for i, tiles in enumerate(key_banks):
                            bank = take(S, "keys", i)
                            for c, t in enumerate(tiles):
                                mm = pe.transpose(bank[0:width(t), c * P:(c + 1) * P],
                                                  pair1[:, k, t * P:t * P + width(t)].bitcast(F32),
                                                  ident[:, :])
                            mm.then_inc(filled, 1)
                    if j == 5 and S.runs("P"):
                        pe.wait_ge(norm_step[2], S.count("P", 5))
                        turn_tokens(S, "norm2", xn[2])
                    if j == 5 and S.runs("E"):
                        pe.wait_ge(norm_step[1], S.count("E", 5))
                        turn_tokens(S, "norm1", xn[1])
                    if j == 6 and S.runs("E"):
                        k = S.ring("E")
                        for h in range(2):
                            bank = take(S, "query", h, after=[use(S, "norm1", h)])
                            two_passes(bank[:, 0:HALF], score_w, 0, P, pair1[:, k, h * HALF:(h + 1) * HALF]
                                       ).then_inc(filled, 1)
                    if j == 6:
                        if S.runs("A"):
                            k = S.ring("A")
                            pe.wait_ge(diag_ready, S.count("A", MAX_GROUPS))
                            for h in range(2):
                                cols = slice(h * HALF, (h + 1) * HALF)
                                bank = take(S, "shifted", h)
                                for part in range(2):
                                    pe.matmul(bank[:, 0:HALF], score_w[part][:, :], pair1[:, k, cols],
                                              start=(part == 0), stop=False)
                                pe.matmul(bank[:, 0:HALF], ones_r[:, :], max_diag[:, cols],
                                          start=False, stop=True).then_inc(filled, 1)
                        if S.runs("B"):
                            attend(S, NT - 1)
                        if S.runs("T"):
                            pe.wait_ge(route_step, S.count("T", ROUTE))
                            for i in range(2):
                                bank = take(S, "weights", i)
                                for g in range(G // 2):
                                    mm = pe.transpose(bank[0:4 * E_, g * ROWS:(g + 1) * ROWS],
                                                      wts_pair[:, i * (G // 2) + g, :],
                                                      ident[0:ROWS, 0:ROWS])
                                mm.then_inc(filled, 1)
                        if S.runs("F"):
                            pe.wait_ge(moe_copied, S.count("F", 2))
                            bank = take(S, "back")
                            pe.matmul(bank[0:ROWS, 0:D], moe_t[:, 0:ROWS], ident[0:D, 0:D],
                                      start=True, stop=True)
                            for g in range(1, G):
                                mm = pe.transpose(bank[0:ROWS, g * D:(g + 1) * D],
                                                  moe_t[:, g * ROWS:(g + 1) * ROWS], ident[0:D, 0:D])
                            mm.then_inc(filled, 1)

            def turn_tokens(S, name, src):
                for i in range(2):
                    bank = take(S, name, i)
                    for g in range(G // 2):
                        c = (i * (G // 2) + g) * D
                        if g == 0:
                            pe.matmul(bank[0:D, 0:ROWS], src[:, c:c + D], ident[0:ROWS, 0:ROWS],
                                      start=True, stop=True)
                        else:
                            mm = pe.transpose(bank[0:D, g * ROWS:(g + 1) * ROWS], src[:, c:c + D],
                                              ident[0:ROWS, 0:ROWS])
                    mm.then_inc(filled, 1)

            run_steps(pe, body)

        @block.scalar
        def _(act):
            act.wait_ge(tok_loaded, 16 * 4)

            def body(S):
                for j in range(NT):
                    if (S.at, j) == PREPARE_AT:
                        act.wait_ge(weights_loaded, 16 * N_LOADS)
                    if j == 0 and S.runs("P"):
                        for h in range(2):
                            u = use(S, "mixed", h)
                            act.wait_ge(filled, u.filled())
                            act.activation(attn_t[:, h * HALF:(h + 1) * HALF],
                                           work[u.bank][0:D + 1, 0:HALF], ACT.Copy
                                           ).then_inc(drained[u.bank], 1)
                    if j == 0 and S.runs("F"):
                        first_relu(S, 0)
                    if S.runs("B"):
                        n = width(j)
                        for h in range(2):
                            u = use(S, "scores_t", j, h)
                            act.wait_ge(filled, u.filled())
                            cols = slice(h * HALF, (h + 1) * HALF)
                            act.activation(probs_hi[0:n, j % 3, cols], work[u.bank][0:n, 0:HALF],
                                           ACT.Exp, scale=SCALE)
                            act.activation(probs[0:n, j % 2, cols], work[u.bank][0:n, 0:HALF],
                                           ACT.Exp, scale=SCALE).then_inc(drained[u.bank], 1)
                    if S.runs("F"):
                        if j < CHUNKS:
                            u = use(S, "hidden2", j)
                            act.wait_ge(filled, u.filled())
                            act.activation(act2[:, j % 2, :], work[u.bank][:, 0:HALF], ACT.Relu,
                                           bias=b2[:, j % PAIRS:j % PAIRS + 1]
                                           ).then_inc(drained[u.bank], 1)
                        if j + 1 < CHUNKS:
                            first_relu(S, j + 1)
                        if j in (PAIRS, NT - 1):
                            h = 0 if j == PAIRS else 1
                            act.wait_ge(chunk_done, S.count("F", 2, h + 1))
                            act.activation(moe_t[:, h * HALF:(h + 1) * HALF], ps_moe[0:D, 0:HALF], ACT.Copy
                                           ).then_inc(moe_copied, 1)
                    if j == 4 and S.runs("T"):
                        act.wait_ge(route_step, S.count("T", ROUTE, EXPO_AT))
                        act.activation(expo[:, :, :], expo[:, :, :], ACT.Exp).then_inc(expo_ready, 1)
                    if j == 5 and S.runs("T"):
                        act.wait_ge(route_step, S.count("T", ROUTE, GAP_AT))
                        act.activation(gap_exp[:, :], gap[:, :], ACT.Exp).then_inc(gap_ready, 1)
                    if j == 0 and S.runs("E"):
                        u = use(S, "embed")
                        act.wait_ge(filled, u.filled())
                        act.activation(embed_t[:, 0:NIMG], work[u.bank][:, 0:NIMG], ACT.Identity,
                                       bias=tok_bias[:, :]).then_inc(drained[u.bank], 1)
                    if j == 0 and S.runs("T"):
                        for h in range(2):
                            u = use(S, "router", h)
                            act.wait_ge(filled, u.filled())
                            act.activation(routed[:, h * HALF:(h + 1) * HALF],
                                           work[u.bank][0:2 * RH, 0:HALF], ACT.Relu
                                           ).then_inc(routed_hi, 1)
                    if j == 1 and S.runs("E"):
                        u = use(S, "tokens")
                        act.wait_ge(filled, u.filled())
                        if S.has("E", RING):
                            act.wait_ge(h2_ready, S.count("E", 1, back=RING))
                        act.activation(h1[:, S.ring("E"), :], work[u.bank][0:ROWS, :], ACT.Copy
                                       ).then_inc(drained[u.bank], 1)
                    if j == 2:
                        if S.runs("X"):
                            u = use(S, "patches")
                            act.wait_ge(filled, u.filled())
                            act.activation(patches[:, :].rearrange("p (r h w) -> p w h r", h=2, w=WP2),
                                           work[u.bank][:, 0:NIMG].rearrange("p (w h r) -> p w h r", h=2, w=WP2),
                                           ACT.Copy).then_inc(patches_ready, 1)
                            act.activation(embed_t[:, NIMG:HALF], work[u.bank][:, NIMG:HALF], ACT.Copy
                                           ).then_inc(drained[u.bank], 1)
                    if j == 5:
                        if S.runs("P"):
                            high_half(S, "P", "norm2", pair2, hi2_ready)
                        if S.runs("E"):
                            high_half(S, "E", "norm1", pair1, hi1_ready)
                    if j == 6:
                        if S.runs("E"):
                            for h in range(2):
                                u = use(S, "query", h)
                                act.wait_ge(filled, u.filled())
                                act.activation(query_hi[:, S.ring("E"), h * HALF:(h + 1) * HALF],
                                               work[u.bank][:, 0:HALF], ACT.Copy
                                               ).then_inc(drained[u.bank], 1)
                    if j == 6:
                        if S.runs("A"):
                            for h in range(2):
                                u = use(S, "shifted", h)
                                act.wait_ge(filled, u.filled())
                                act.activation(shifted[0][:, S.ring("A"), h * HALF:(h + 1) * HALF],
                                               work[u.bank][:, 0:HALF], ACT.Copy).then_inc(shifted_hi, 1)
                        if S.runs("B"):
                            for h in range(2):
                                act.wait_ge(attended, S.count("B", 2 * NT, 2 * NT - 1 + h))
                                act.activation(blend_t[:, h * HALF:(h + 1) * HALF],
                                               ps_attn[:, h, 0:HALF], ACT.Copy
                                               ).then_inc(blend_copied, 1)
                        if S.runs("T"):
                            for h in range(2):
                                u = use(S, "weights", h)
                                act.wait_ge(filled, u.filled())
                                act.activation(weights_t[:, S.ring("T"), h * HALF:(h + 1) * HALF],
                                               work[u.bank][0:4 * E_, 0:HALF], ACT.Copy
                                               ).then_inc(drained[u.bank], 1)

            def first_relu(S, c):
                u = use(S, "hidden1", c)
                act.wait_ge(filled, u.filled())
                act.activation(act1[:, c % 2, :], work[u.bank][:, 0:HALF], ACT.Relu
                               ).then_inc(drained[u.bank], 1)

            def high_half(S, stage, name, pair, hi_ready):
                for h in range(2):
                    u = use(S, name, h)
                    act.wait_ge(filled, u.filled())
                    act.activation(pair[0:D, S.ring(stage), h * HALF:(h + 1) * HALF],
                                   work[u.bank][0:D, 0:HALF], ACT.Copy, bias=1.0 / D).then_inc(hi_ready, 1)

            run_steps(act, body)

        @block.vector
        def _(dve):
            made = 0

            def prep(instruction):
                nonlocal made
                made += 1
                instruction.then_inc(prep_copied, 1)

            dve.wait_ge(consts_made, N_CONSTS)
            dve.wait_ge(prep_filled, 1)
            for k in range(2):
                r = slice(k * D, (k + 1) * D)
                prep(dve.tensor_copy(embed_w[r, r], ps_moe[r, 0:D]))

            def prepare():
                dve.wait_ge(weights_loaded, 16 * N_LOADS)
                dve.wait_ge(prep_filled, 2)
                prep(dve.tensor_copy(query_t[:, :], ps_moe[0:D, P:2 * P]))
                prep(dve.tensor_copy(key_t[:, :], ps_moe[0:D, 2 * P:3 * P]))
                dve.wait_ge(prep_filled, 3)
                prep(dve.tensor_copy(score_w[0][:, :], ps_moe[:, 3 * P:4 * P]))
                dve.wait_ge(prep_copied, made)
                prep(dve.tensor_tensor(score_w[1][:, :], ps_moe[:, 3 * P:4 * P], score_w[0][:, :].bitcast(F32),
                                       ALU.subtract))
                prep(dve.tensor_copy(value_w[:, 0:D], ps_attn[:, 0, VC:VC + D]))
                for i, (c, n) in enumerate(((0, EC), (EC, NF - EC))):
                    prep(dve.tensor_copy(first_w[0][:, c:c + n], ps_attn[:, i, 0:n]))
                    dve.wait_ge(prep_copied, made)
                    prep(dve.tensor_tensor(first_w[1][:, c:c + n], ps_attn[:, i, 0:n],
                                           first_w[0][:, c:c + n].bitcast(F32), ALU.subtract))
                prep(dve.tensor_copy(router2[:, 0:E_], raw_r2[:, :]))
                prep(dve.tensor_copy(b3_hi[:, :], raw_b3[:, :]))
                prep(dve.tensor_scalar(is_lo_row[:, :], is_hi_row[:, :], -1.0, 1.0, ALU.mult, ALU.add))
                prep(dve.tensor_copy(pick[:, :], raw_pick[:, :, :, :].rearrange("p q k d -> p (q k d)")))
                prep(dve.tensor_scalar(ones_r[:, :], ident[:, :], 0.0, 1.0, ALU.mult, ALU.add))
                dve.wait_ge(prep_copied, made)
                prep(dve.tensor_tensor(router2[:, E_:2 * E_], raw_r2[:, :], router2[:, 0:E_].bitcast(F32),
                                       ALU.subtract))
                prep(dve.tensor_tensor(b3_lo[:, :], raw_b3[:, :], b3_hi[:, :].bitcast(F32), ALU.subtract))
                dve.wait_ge(prep_copied, made)
                prep(dve.tensor_tensor(b3_low_rows[:, :], b3_lo[:, :], is_lo_row[:, :], ALU.mult))
                prep(dve.tensor_tensor(raw_b3[:, :], b3_hi[:, :].bitcast(F32), is_hi_row[:, :], ALU.mult))
                dve.wait_ge(prep_copied, made)
                prep(dve.tensor_tensor(b3[:, :], raw_b3[:, :], b3_low_rows[:, :], ALU.add))
                assert made == N_PREP

            def low_half(S, stage, name, pair, hi_ready):
                for h in range(2):
                    u = use(S, name, h)
                    cols = slice(h * HALF, (h + 1) * HALF)
                    dve.wait_ge(hi_ready, S.count(stage, 2, h + 1))
                    dve.scalar_tensor_tensor(out=pair[D:P, S.ring(stage), cols], in0=work[u.bank][0:D, 0:HALF],
                                             scalar=1.0 / D, in1=pair[0:D, S.ring(stage), cols].bitcast(F32),
                                             op0=ALU.add, op1=ALU.subtract
                                             ).then_inc(drained[u.bank], 1)

            def sum_tokens(S, stage, k, src):
                if S.has(stage, 1):
                    dve.wait_ge(norm_step[k], S.count(stage, 5, 1, back=1))
                dve.tensor_reduce(stat[k][0][:, :], groups(src), AX.X, ALU.add).then_inc(total_ready[k], 1)

            def variance(S, stage, k):
                _, _, squares, var, _ = stat[k]
                step = var_step[k]
                dve.wait_ge(norm_step[k], S.count(stage, 5, 3))
                dve.tensor_reduce(squares[:, :], groups(sq[k][:, :]), AX.X, ALU.add).then_inc(step, 1)
                dve.wait_ge(step, S.count(stage, 2, 1))
                dve.tensor_scalar(var[:, :], squares[:, :], 1.0 / D, EPS, ALU.mult, ALU.add).then_inc(step, 1)

            many = [ROWS, G, E_]

            def read_logits(S):
                if S.has("T", 1):
                    dve.wait_ge(route_step, S.count("T", ROUTE, back=1))
                u = use(S, "logits")
                dve.wait_ge(filled, u.filled())
                logits = work[u.bank][0:ROWS, 0:2 * E_ * G].rearrange("p (g e) -> p g e", e=2 * E_)
                dve.tensor_tensor(lg_hi[:, :, :], logits[:, :, 0:E_],
                                  router_bias[:, :].unsqueeze(1).broadcast_to(many), ALU.add
                                  ).then_inc(route_step, 1)
                dve.wait_ge(route_step, S.count("T", ROUTE, 1))
                dve.tensor_tensor(lg[:, :, :], lg_hi[:, :, :], logits[:, :, E_:2 * E_], ALU.add
                                  ).then_inc(drained[u.bank], 1)

            def router(S, k):
                if k == 1:
                    wait_read(dve, use(S, "logits"))
                else:
                    dve.wait_ge(route_step, S.count("T", ROUTE, k))
                n = 0 if k < 7 else 1
                left = (lg, lg_rest)[n]
                both = [ROWS, G, 2, E_]
                pairs = wts_pair[:, :, :].rearrange("p g (k e) -> p g k e", k=2)
                high = wts_hi[:, :, :].bitcast(F32).unsqueeze(2).broadcast_to(both)
                if k in (1, 7):
                    done = dve.tensor_reduce(best[:, n, :], left[:, :, :], AX.X, ALU.max)
                elif k in (2, 8):
                    done = dve.tensor_tensor(tie[:, :, :], left[:, :, :], wide(best[:, n, :], E_), ALU.is_equal)
                elif k in (3, 9):
                    done = dve.tensor_tensor(tie[:, :, :], tie[:, :, :],
                                             prio[0:ROWS, :].unsqueeze(1).broadcast_to(many), ALU.mult)
                elif k in (4, 10):
                    done = dve.tensor_reduce(first_tie[:, :], tie[:, :, :], AX.X, ALU.max)
                elif k in (5, 11):
                    done = dve.tensor_tensor(chosen[:, n, :, :], tie[:, :, :], wide(first_tie[:, :], E_),
                                             ALU.is_equal)
                elif k == 6:
                    done = dve.scalar_tensor_tensor(out=lg_rest[:, :, :], in0=chosen[:, 0, :, :],
                                                    scalar=-BIG, in1=lg[:, :, :], op0=ALU.mult, op1=ALU.add)
                elif k == 12:
                    done = dve.tensor_tensor(expo[:, :, 0:E_], lg[:, :, :], wide(best[:, 0, :], E_),
                                             ALU.subtract)
                elif k == 13:
                    done = dve.tensor_tensor(expo[:, :, E_], best[:, 1, :], best[:, 0, :], ALU.subtract)
                elif k == EXPO_AT:
                    dve.wait_ge(expo_ready, S.count("T", 1))
                    done = dve.tensor_reduce(expo_sum[:, :], expo[:, :, 0:E_], AX.X, ALU.add)
                elif k == 15:
                    done = dve.reciprocal(expo_inv[:, :], expo_sum[:, :])
                elif k == 16:
                    done = dve.scalar_tensor_tensor(out=gap[:, :], in0=expo[:, :, E_], scalar=1.0,
                                                    in1=expo_inv[:, :], op0=ALU.subtract, op1=ALU.mult)
                elif k == GAP_AT:
                    dve.wait_ge(gap_ready, S.count("T", 1))
                    done = dve.tensor_scalar(gap[:, :], gap_exp[:, :], 1.0, None, ALU.add)
                elif k == 18:
                    done = dve.reciprocal(share[:, 0, :], gap[:, :])
                elif k == 19:
                    done = dve.tensor_tensor(share[:, 1, :], gap_exp[:, :], share[:, 0, :], ALU.mult)
                elif k == 20:
                    done = dve.tensor_tensor(wsum[:, :, :, :], chosen[:, :, :, :],
                                             share[:, :, :].unsqueeze(3).broadcast_to([ROWS, 2, G, E_]),
                                             ALU.mult)
                elif k == 21:
                    done = dve.tensor_tensor(wts[:, :, :], wsum[:, 0, :, :], wsum[:, 1, :, :], ALU.add)
                elif k == 22:
                    done = dve.tensor_copy(wts_hi[:, :, :], wts[:, :, :])
                elif k == 23:
                    done = dve.tensor_copy(pairs[:, :, :, 0:E_], high)
                else:
                    done = dve.tensor_tensor(pairs[:, :, :, E_:2 * E_],
                                             wts[:, :, :].unsqueeze(2).broadcast_to(both), high, ALU.subtract)
                done.then_inc(route_step, 1)

            router_at = {
                (2, "start"): (1,), (2, "max0"): (2,), (2, "max1"): (3,), (2, "low"): (4,), (2, "scaled"): (5,),
                (2, "end"): (6,),
                (3, "start"): (7,), (3, "max0"): (8,), (3, "max1"): (9,), (3, "low"): (10,),
                (3, "scaled"): (11,), (3, "end"): (12,),
                (4, "start"): (13,), (4, "scaled"): (14,), (4, "end"): (15,),
                (5, "start"): (16,), (5, "scaled"): (17,), (5, "low_half0"): (18,), (5, "low_half1"): (19,),
                (5, "end"): (20,),
                (6, "start"): (21, 22), (6, "low"): (23, 24),
            }

            def route(S, j, place):
                if S.runs("T"):
                    for k in router_at.get((j, place), ()):
                        router(S, k)

            def body(S):
                for j in range(NT):
                    if (S.at, j) == PREPARE_AT:
                        prepare()
                    if j == 2 and S.runs("E"):
                        wait_read(dve, use(S, "tokens"))
                        sum_tokens(S, "E", 1, h1[:, S.ring("E"), :])
                    route(S, j, "start")
                    if S.runs("A"):
                        for t in score_tiles(j):
                            n = width(t)
                            for h in range(2):
                                u = use(S, "scores", t, h)
                                dve.wait_ge(filled, u.filled())
                                dve.tensor_reduce(row_max[0:n, t, h:h + 1], work[u.bank][0:n, 0:HALF],
                                                  AX.X, ALU.max).then_inc(drained[u.bank], 1)
                                route(S, j, f"max{h}")
                    else:
                        route(S, j, "max0")
                        route(S, j, "max1")
                    if S.runs("B"):
                        low_probs(dve, S, j, 0)
                    route(S, j, "low")
                    if j < CHUNKS and S.runs("F"):
                        u = use(S, "spread", j)
                        dve.wait_ge(filled, u.filled())
                        wait_read(dve, use(S, "hidden2", j))
                        dve.tensor_tensor(scaled[:, j % 2, :], act2[:, j % 2, :], work[u.bank][:, 0:HALF],
                                          ALU.mult).then_inc(drained[u.bank], 1)
                    route(S, j, "scaled")
                    if j == 0 and S.runs("P"):
                        halves = []
                        for i in range(2):
                            u = use(S, "attn", i)
                            gs = slice(i * (G // 2), (i + 1) * (G // 2))
                            src = work[u.bank][0:ROWS, 0:(G // 2) * (D + 1)].rearrange(
                                "p (g d) -> p g d", d=D + 1)
                            dve.wait_ge(filled, u.filled())
                            dve.reciprocal(inv_sum[:, gs], src[:, :, D]).then_inc(sums_inverted, 1)
                            halves.append((u, gs, src))
                        if S.has("P", 1):
                            dve.wait_ge(h2_ready, S.count("P", 1, back=1))
                        for i, (u, gs, src) in enumerate(halves):
                            dve.wait_ge(sums_inverted, S.count("P", 2, i + 1))
                            dve.tensor_tensor(groups(attn[:, :])[:, gs, :], src[:, :, 0:D],
                                              wide(inv_sum[:, :])[:, gs, :], ALU.mult
                                              ).then_inc(drained[u.bank], 1)
                    if j == 0 and S.runs("T"):
                        for h in range(2):
                            u = use(S, "router", h)
                            cols = slice(h * HALF, (h + 1) * HALF)
                            dve.wait_ge(routed_hi, S.count("T", 2, h + 1))
                            dve.scalar_tensor_tensor(out=routed[RH:2 * RH, cols],
                                                     in0=work[u.bank][RH:2 * RH, 0:HALF], scalar=0.0,
                                                     in1=routed[RH:2 * RH, cols].bitcast(F32),
                                                     op0=ALU.max, op1=ALU.subtract
                                                     ).then_inc(drained[u.bank], 1)
                    if j == 1 and S.runs("P"):
                        for i in range(2):
                            wait_read(dve, use(S, "attn", i))
                        dve.tensor_tensor(h2[:, S.ring("P"), :], attn[:, :], h1[:, S.ring("P"), :],
                                          ALU.add).then_inc(h2_ready, 1)
                    if j == 1 and S.runs("X"):
                        k = S.ring("X")
                        dve.wait_ge(pixels_loaded[k], 2 * S.ring_dma("X"))
                        if S.has("X", 1):
                            dve.wait_ge(patches_ready, S.count("X", 1, back=1))
                        dve.tensor_copy(by_patch[:, :].rearrange("r (w p q) -> r p w q", p=PATCH, q=PATCH),
                                        pixels[:, k, :].rearrange("r (p w q) -> r p w q", p=PATCH, q=PATCH)
                                        ).then_inc(by_patch_ready, 1)
                    if j == 1 and S.runs("P"):
                        dve.wait_ge(h2_ready, S.count("P", 1))
                        sum_tokens(S, "P", 2, h2[:, S.ring("P"), :])
                    if j == 2 and S.runs("P"):
                        variance(S, "P", 2)
                    if j == 1 and S.runs("T"):
                        read_logits(S)
                    if j == 4 and S.runs("A"):
                        k = S.ring("A")
                        for i, tiles in enumerate(key_banks):
                            u = use(S, "keys", i)
                            whole = [t for t in tiles if width(t) == P]
                            first, n = tiles[0], len(whole)
                            dve.wait_ge(filled, u.filled())
                            copied = dve.tensor_copy(
                                keys[:, k, first:first + n, :],
                                work[u.bank][:, 0:n * P].rearrange("p (t d) -> p t d", d=P))
                            for t in tiles:
                                if t not in whole:
                                    copied = dve.tensor_copy(keys[0:width(t), k, t, :],
                                                             work[u.bank][0:width(t), n * P:(n + 1) * P])
                            copied.then_inc(drained[u.bank], 1)
                    if j == 3 and S.runs("E"):
                        variance(S, "E", 1)
                    if j == 5:
                        if S.runs("P"):
                            low_half(S, "P", "norm2", pair2, hi2_ready)
                        route(S, j, "low_half0")
                        if S.runs("E"):
                            low_half(S, "E", "norm1", pair1, hi1_ready)
                        route(S, j, "low_half1")
                    if S.runs("A"):
                        for tiles in max_tiles(j):
                            t, m, n = tiles[0], len(tiles), width(tiles[0])
                            wait_read(dve, use(S, "scores", tiles[-1], 1))
                            if t == 0 and S.has("A", 1):
                                dve.wait_ge(diag_ready, S.count("A", MAX_GROUPS, back=1))
                            dve.tensor_reduce(minus_max[0:n, t:t + m], row_max[0:n, t:t + m, :], AX.X, ALU.max,
                                              negate=True).then_inc(max_ready, 1)
                    route(S, j, "end")
                    if j == 6:
                        if S.runs("A"):
                            for h in range(2):
                                u = use(S, "shifted", h)
                                cols = slice(h * HALF, (h + 1) * HALF)
                                k = S.ring("A")
                                dve.wait_ge(shifted_hi, S.count("A", 2, h + 1))
                                dve.tensor_tensor(shifted[1][:, k, cols], work[u.bank][:, 0:HALF],
                                                  shifted[0][:, k, cols].bitcast(F32), ALU.subtract
                                                  ).then_inc(drained[u.bank], 1)
                        if S.runs("F"):
                            u = use(S, "back")
                            k = S.ring("F")
                            dve.wait_ge(filled, u.filled())
                            if S.has("F", RING):
                                dve.wait_ge(stored[k], S.ring_dma("F", back=RING))
                            dve.tensor_tensor(result[:, k, :], work[u.bank][0:ROWS, :], h2[:, k, :], ALU.add
                                              ).then_inc(drained[u.bank], 1)

            run_steps(dve, body)

    return nc


_INS = ["x", "txt", "L0_tok_W", "L0_tok_b", "L0_attn_Wq", "L0_attn_bq", "L0_attn_Wk", "L0_attn_bk",
        "L0_attn_Wv", "L0_attn_bv", "L0_ffn_router_w1", "L0_ffn_router_b1", "L0_ffn_router_w2",
        "L0_ffn_router_b2", "L0_ffn_expert_w1", "L0_ffn_expert_b1", "L0_ffn_expert_w2",
        "L0_ffn_expert_b2", "L0_ffn_expert_w3", "L0_ffn_expert_b3"]


def kernel(**inputs):
    import numpy as np
    import concourse.bacc as bacc
    from concourse.bass_utils import run_bass_kernel_spmd

    nc = bacc.Bacc("TRN2", target_bir_lowering=False, num_devices=1)
    arrays, args = {}, []
    for name in _INS:
        a = np.ascontiguousarray(inputs[name])
        arrays[f"in_{name}"] = a
        args.append(nc.dram_tensor(f"in_{name}", a.shape, mybir.dt.from_np(a.dtype), kind="ExternalInput").ap())
    out = nc.dram_tensor("out", (BATCH, TOK, D), F32, kind="ExternalOutput").ap()
    encoder_kernel(nc, *args, out)
    r = run_bass_kernel_spmd(nc, [arrays], core_ids=[0])
    return r.results[0]["out"]
```
